# Optimizing a Trainium2 kernel written in Bass

```python
import numpy as np
import jax
import jax.numpy as jnp

def _softmax(x, axis=-1):
    return jax.nn.softmax(x, axis=axis)

def _gelu(x):
    return jax.nn.gelu(x, approximate=True)

def _silu(x):
    return jax.nn.silu(x)

def _sigmoid(x):
    return jax.nn.sigmoid(x)

def _layernorm(x, axis=-1, eps=1e-05):
    m = jnp.mean(x, axis=axis, keepdims=True)
    v = jnp.var(x, axis=axis, keepdims=True)
    return (x - m) / jnp.sqrt(v + eps)

def _scatter_add(tgt, idx, src, axis=0):
    return tgt.at[idx].add(src)

def _segment_sum(src, seg, n):
    return jax.ops.segment_sum(src, seg, n)
kernel_name = 'mk_decoder_postln_d1_seqx_r4_3c8a14'

def setup_inputs(seed: int=0):
    np.random.seed(seed)
    _w = jnp.asarray

    def _rec_inputs():
        import jax
        import jax.numpy as jnp
        _rk = jax.random.key(seed)
        x = -0.0003929 + 0.9999 * jax.random.normal(jax.random.fold_in(_rk, 1), (16, 128, 256), jnp.float32)
        _lenS = 128 - jax.random.randint(jax.random.fold_in(_rk, 7), (16,), 0, max(1, 128 // 4) + 1, jnp.int32)
        _lenS2 = 128 - jax.random.randint(jax.random.fold_in(_rk, 8), (16,), 0, max(1, 128 // 4) + 1, jnp.int32)
        _ctx_1024P = jax.random.normal(jax.random.fold_in(_rk, 11), (16, 16, 256), jnp.float32)
        _ctx_1024c = jax.random.dirichlet(jax.random.fold_in(_rk, 511), 0.3 * jnp.ones((16,), jnp.float32), (16, 128))
        _ctx_1024t = jnp.einsum('bsk,bkd->bsd', _ctx_1024c, _ctx_1024P)
        _ctx_1024t = _ctx_1024t * jax.lax.rsqrt(jnp.mean(jnp.square(_ctx_1024t)) + 1e-12) * 0.953939
        ctx_1024 = 2.81802e-05 + 1.00001 * (_ctx_1024t + 0.3 * jax.random.normal(jax.random.fold_in(_rk, 611), (16, 128, 256), jnp.float32))
        return (x, ctx_1024)
    x, ctx_1024 = _rec_inputs()

    def _L0_attn_setup():
        import jax, jax.numpy as jnp
        import numpy as np
        EMBED = 256
        N_HEAD = 16
        HEAD_DIM = EMBED // N_HEAD
        key = jax.random.key(seed)
        ks = jax.random.split(key, 9)

        def xavier(k, shape, fan_in, fan_out):
            bound = float(np.sqrt(6.0 / (fan_in + fan_out)))
            return jax.random.uniform(k, shape, jnp.float32, -bound, bound)
        x = jax.random.normal(ks[0], (4, 512, EMBED), jnp.float32)
        wq = xavier(ks[1], (N_HEAD, EMBED, HEAD_DIM), EMBED, HEAD_DIM)
        wk = xavier(ks[2], (N_HEAD, EMBED, HEAD_DIM), EMBED, HEAD_DIM)
        wv = xavier(ks[3], (N_HEAD, EMBED, HEAD_DIM), EMBED, HEAD_DIM)
        bq = jnp.zeros((N_HEAD, 1, HEAD_DIM), jnp.float32)
        bk = jnp.zeros((N_HEAD, 1, HEAD_DIM), jnp.float32)
        bv = jnp.zeros((N_HEAD, 1, HEAD_DIM), jnp.float32)
        bnd = 1.0 / float(np.sqrt(EMBED))
        wo = jax.random.uniform(ks[4], (EMBED, EMBED), jnp.float32, -bnd, bnd)
        bo = jax.random.uniform(ks[5], (EMBED,), jnp.float32, -bnd, bnd)
        return {'x': x, 'wq': wq, 'bq': bq, 'wk': wk, 'bk': bk, 'wv': wv, 'bv': bv, 'wo': wo, 'bo': bo}
    _L0_attn_all = _L0_attn_setup()
    _L0_attn_in = {k: v for k, v in _L0_attn_all.items() if k in ('wq', 'bq', 'wk', 'bk', 'wv', 'bv', 'wo', 'bo')}
    del _L0_attn_all

    def _L0_xattn_setup():
        import jax, jax.numpy as jnp
        import numpy as np
        B, T, D = (8, 512, 256)
        key = jax.random.key(seed)
        k1, k2, k3, k4 = jax.random.split(key, 4)
        k = jax.random.normal(k1, (B, T, D), dtype=jnp.float32)
        v = jax.random.normal(k2, (B, T, D), dtype=jnp.float32)
        w = jax.random.uniform(k3, (D,), dtype=jnp.float32, minval=0.0005, maxval=0.008)
        u = 0.1 * jax.random.normal(k4, (D,), dtype=jnp.float32)
        return {'k': k, 'v': v, 'w': w, 'u': u}
    _L0_xattn_all = _L0_xattn_setup()
    _L0_xattn_in = {k: v for k, v in _L0_xattn_all.items() if k in ('w', 'u')}
    del _L0_xattn_all

    def _L0_ffn_setup():
        import jax, jax.numpy as jnp
        import numpy as np
        B, S, H, E, K, F = (4, 512, 256, 8, 128, 1024)
        key = jax.random.key(seed)
        k0, k1, k2, k3 = jax.random.split(key, 4)
        sc = lambda d: 1.0 / np.sqrt(d).astype(np.float32)
        return {'x': jax.random.normal(k0, (B, S, H), jnp.float32), 'Wg': jax.random.normal(k1, (E, H), jnp.float32) * sc(H), 'W1': jax.random.normal(k2, (E, H, F), jnp.float32) * sc(H), 'b1': jnp.zeros((E, F), jnp.float32), 'W2': jax.random.normal(k3, (E, F, H), jnp.float32) * sc(F), 'b2': jnp.zeros((E, H), jnp.float32)}
    _L0_ffn_all = _L0_ffn_setup()
    _L0_ffn_in = {k: v for k, v in _L0_ffn_all.items() if k in ('Wg', 'W1', 'b1', 'W2', 'b2')}
    del _L0_ffn_all
    return {'x': x, 'ctx_1024': ctx_1024, 'L0_attn_wq': _L0_attn_in['wq'], 'L0_attn_bq': _L0_attn_in['bq'], 'L0_attn_wk': _L0_attn_in['wk'], 'L0_attn_bk': _L0_attn_in['bk'], 'L0_attn_wv': _L0_attn_in['wv'], 'L0_attn_bv': _L0_attn_in['bv'], 'L0_attn_wo': _L0_attn_in['wo'], 'L0_attn_bo': _L0_attn_in['bo'], 'L0_xattn_w': _L0_xattn_in['w'], 'L0_xattn_u': _L0_xattn_in['u'], 'L0_ffn_Wg': _L0_ffn_in['Wg'], 'L0_ffn_W1': _L0_ffn_in['W1'], 'L0_ffn_b1': _L0_ffn_in['b1'], 'L0_ffn_W2': _L0_ffn_in['W2'], 'L0_ffn_b2': _L0_ffn_in['b2']}

def reference(x, ctx_1024, L0_attn_wq, L0_attn_bq, L0_attn_wk, L0_attn_bk, L0_attn_wv, L0_attn_bv, L0_attn_wo, L0_attn_bo, L0_xattn_w, L0_xattn_u, L0_ffn_Wg, L0_ffn_W1, L0_ffn_b1, L0_ffn_W2, L0_ffn_b2):
    import jax
    import jax.numpy as jnp

    def _L0_attn_ref(x, wq, bq, wk, bk, wv, bv, wo, bo):
        import jax, jax.numpy as jnp
        import numpy as np
        EMBED = 256
        N_HEAD = 16
        HEAD_DIM = EMBED // N_HEAD
        q = jnp.einsum('bsd,hde->bhse', x, wq) + bq
        k = jnp.einsum('bsd,hde->bhse', x, wk) + bk
        v = jnp.einsum('bsd,hde->bhse', x, wv) + bv
        scale = 1.0 / jnp.sqrt(jnp.asarray(q.shape[-1], q.dtype))
        scores = jax.nn.softmax(jnp.einsum('bhse,bhte->bhst', q, k) * scale, axis=-1)
        att = jnp.einsum('bhst,bhte->bhse', scores, v)
        b, h, s, e = att.shape
        att = att.transpose(0, 2, 1, 3).reshape(b, s, h * e)
        return att @ wo.T + bo

    def _L0_xattn_ref(k, v, w, u):
        import jax, jax.numpy as jnp
        import numpy as np
        B, T, D = (8, 512, 256)
        Tn = k.shape[-2]
        kt = jnp.moveaxis(k, -2, 0)
        vt = jnp.moveaxis(v, -2, 0)
        ed = jnp.exp(-w)
        eg = jnp.exp(w)

        def step(carry, xs):
            A, Bm = carry
            kk, vv, t = xs
            out = A + jnp.exp(u + kk) * (vv * Bm + jnp.maximum(t - 1.0, 0.0))
            inc = jnp.where(t == 0.0, 0.0, 1.0)
            A = ed * A + inc * jnp.exp(kk) * vv
            Bm = eg * Bm + inc * jnp.exp(-kk)
            return ((A, Bm), out)
        A0 = jnp.zeros_like(kt[0])
        B0 = jnp.zeros_like(kt[0])
        ts = jnp.arange(Tn, dtype=k.dtype)
        (_, _), out = jax.lax.scan(step, (A0, B0), (kt, vt, ts))
        return jnp.moveaxis(out, 0, -2)

    def _L0_ffn_ref(x, Wg, W1, b1, W2, b2):
        import jax, jax.numpy as jnp
        import numpy as np
        B, S, H, E, K, F = (4, 512, 256, 8, 128, 1024)
        b, s, h = x.shape
        logits = jnp.einsum('bsh,eh->bse', x, Wg)
        Sm = jnp.swapaxes(jax.nn.softmax(logits, axis=-1), 1, 2)
        G, I = jax.lax.top_k(Sm, K)
        ex = jnp.take_along_axis(x[:, None, :, :], I[..., None], axis=2)
        h1 = jax.nn.gelu(jnp.einsum('bekh,ehf->bekf', ex, W1) + b1[None, :, None, :])
        out = jnp.einsum('bekf,efh->bekh', h1, W2) + b2[None, :, None, :]
        out = G[..., None] * out
        new_x = jnp.zeros_like(x).at[jnp.arange(b)[:, None, None], I].add(out)
        return new_x
    x = _layernorm(x + _L0_attn_ref(x, L0_attn_wq, L0_attn_bq, L0_attn_wk, L0_attn_bk, L0_attn_wv, L0_attn_bv, L0_attn_wo, L0_attn_bo), axis=-1)
    x = _layernorm(x + _L0_xattn_ref(x, ctx_1024, L0_xattn_w, L0_xattn_u), axis=-1)
    x = _layernorm(x + _L0_ffn_ref(x, L0_ffn_Wg, L0_ffn_W1, L0_ffn_b1, L0_ffn_W2, L0_ffn_b2), axis=-1)
    return x

_drawn_inputs = setup_inputs


def setup_inputs(seed=0):
    import zlib

    import numpy as np

    out = dict(_drawn_inputs(seed))
    spreads = {'L0_attn_bq': (0.0, 0.368),
     'L0_attn_bk': (0.0, 0.8),
     'L0_attn_bv': (0.0, 0.276),
     'L0_ffn_b1': (0.0, 0.1),
     'L0_ffn_b2': (0.0, 0.1)}
    factors = {'L0_attn_bo': 2.894}
    for name, (base, spread) in spreads.items():
        noise = np.random.default_rng([zlib.crc32(name.encode()), seed]).standard_normal(out[name].shape)
        drawn = base * np.exp(spread * noise) if base else spread * noise
        out[name] = jnp.asarray(drawn.astype(out[name].dtype))
    for name, factor in factors.items():
        out[name] = (out[name] * factor).astype(out[name].dtype)
    return out
```

```python
from contextlib import ExitStack

import concourse.bass as bass
from concourse import mybir

F32 = mybir.dt.float32
F32R = mybir.dt.float32r
F16 = mybir.dt.float16
BF16 = mybir.dt.bfloat16
ALU = mybir.AluOpType
ACT = mybir.ActivationFunctionType
AX_X = mybir.AxisListType.X

P = 128
EPS = 1e-5


def decoder_layer(nc, x, ctx_in, wq, wk, wv, wo, cols, bv, bo, wg, w1, b1, w2, b2, out):
    B, S, D = x.shape
    E, _, F = w1.shape
    H = 16
    DH = D // H
    C = D // P
    HC = H // C
    HQ = HC // 2
    FC = F // P
    PAIR = 2
    BLK = 4
    NPAIR = B // PAIR
    NBLK = B // BLK
    TOK = BLK * S
    VW = DH + 1
    QUADS = PAIR * C * 2
    UNITS = PAIR * C
    SC = 4
    SLOTS = FC + BLK
    STEPS = SC * SLOTS
    PIECES = 4
    PW = C * F // PIECES
    assert S == P and C == 2 and DH == 16 and TOK == 512 and E == 2 * SC

    with ExitStack() as ctx:
        def sb(name, shape, dt=F32):
            return ctx.enter_context(nc.sbuf_tensor(name, shape, dt))

        def sem(name):
            return ctx.enter_context(nc.semaphore(name))

        ident = sb("ident", [P, P])
        head_mask = sb("head_mask", [P, HC])
        ramp = sb("ramp", [P, S])
        ones = sb("ones", [P, S])
        proj_hi = sb("proj_hi", [P, 4, C, D], F32R)
        proj_lo = sb("proj_lo", [P, 4, C, D], F32R)
        bqk = sb("bqk", [P, 2, C])
        bq_scaled = sb("bq_scaled", [P, C])
        bv_all = sb("bv_all", [P, D])
        bo_all = sb("bo_all", [P, D])
        wu = sb("wu", [P, 2, C])
        decay = sb("decay", [P, 2, C])
        decay_row = sb("decay_row", [P, 2, C, S])
        wg_raw = sb("wg_raw", [P, C, E])
        wg_hi = sb("wg_hi", [P, C, P], F32R)
        wg_lo = sb("wg_lo", [P, C, P], F32R)
        b1_all = sb("b1_all", [P, E * FC])
        b2_raw = sb("b2_raw", [E, D])
        b2_hi = sb("b2_hi", [E, D], F32R)
        b2_lo = sb("b2_lo", [E, D], F32R)
        power = sb("power", [P, BLK])
        eps_row = sb("eps_row", [P, BLK])

        x_in = sb("x_in", [P, PAIR, D])
        ctx_sb = sb("ctx_sb", [P, PAIR, D])
        x_bo = sb("x_bo", [P, PAIR, D])
        xt_hi = sb("xt_hi", [P, C, PAIR * S], F32R)
        xt_lo = sb("xt_lo", [P, C, PAIR * S], F32R)
        q_all = sb("q_all", [P, C, PAIR * S])
        q_hi = sb("q_hi", [P, C, PAIR * S], F32R)
        q_lo = sb("q_lo", [P, C, PAIR * S], F32R)
        k_all = sb("k_all", [P, C, PAIR * S])
        k_hi = sb("k_hi", [P, C, PAIR * S], F32R)
        k_rest = sb("k_rest", [P, C, PAIR * S])
        kd_hi = sb("kd_hi", [P, PAIR, HC, S], F32R)
        kd_lo = sb("kd_lo", [P, PAIR, HC, S], F32R)
        v_all = sb("v_all", [P, PAIR, D])
        v_hi = sb("v_hi", [P, PAIR, H, VW], BF16)
        v_mid = sb("v_mid", [P, PAIR, H, VW], BF16)
        v_lo = sb("v_lo", [P, PAIR, H, VW], BF16)
        neg_max = sb("neg_max", [P, QUADS, HQ])
        probs = sb("probs", [P, 2, 2, HQ, S])
        pt_hi = sb("pt_hi", [P, 2, HQ, S], F16)
        pt_lo = sb("pt_lo", [P, 2, HQ, S], F16)
        inv_sum = sb("inv_sum", [P, UNITS, HC])
        att = sb("att", [P, PAIR, D])
        y1 = sb("y1", [P, PAIR, D])
        stats = sb("stats", [P, BLK, 6])
        moments = sb("moments", [P, 3, BLK, 2])
        spare = sb("spare", [P, 3])
        var_eps = sb("var_eps", [P, 3, BLK])
        rstd = sb("rstd", [P, 3, BLK])
        y1t = sb("y1t", [P, C, PAIR, S])
        ctx_t = sb("ctx_t", [P, C, PAIR, S])
        exp_k = sb("exp_k", [P, C, PAIR, S])
        exp_uk = sb("exp_uk", [P, C, PAIR, S])
        inc_a = sb("inc_a", [P, C, PAIR, S])
        inc_b = sb("inc_b", [P, C, PAIR, S])
        x2 = sb("x2", [P, BLK, D])

        x2t_hi = sb("x2t_hi", [P, C, TOK], F32R)
        x2t_lo = sb("x2t_lo", [P, C, TOK], F32R)
        logits_t = sb("logits_t", [P, TOK])
        logits = sb("logits", [P, BLK, E])
        route_exps = sb("route_exps", [P, BLK, E])
        route_max = sb("route_max", [P, BLK])
        route_sum = sb("route_sum", [P, BLK])
        route_inv = sb("route_inv", [P, BLK])
        gate = sb("gate", [P, BLK, E])
        gt_hi = sb("gt_hi", [E, TOK], F32R)
        gt_lo = sb("gt_lo", [E, TOK], F32R)
        w1_raw = sb("w1_raw", [P, C * F])
        w2_raw = sb("w2_raw", [P, C * F])
        w1_hi = sb("w1_hi", [P, C * F], F32R)
        w1_lo = sb("w1_lo", [P, C * F], F32R)
        w2_hi = sb("w2_hi", [P, C * F], F32R)
        w2_lo = sb("w2_lo", [P, C * F], F32R)
        h_all = sb("h_all", [P, 2, TOK])
        h_hi = sb("h_hi", [P, FC, TOK], F32R)
        h_lo = sb("h_lo", [P, FC, TOK], F32R)
        acc = sb("acc", [P, BLK, D])

        w1h = w1_hi[:].rearrange("p (c f) -> p c f", c=C)
        w1l = w1_lo[:].rearrange("p (c f) -> p c f", c=C)
        w2h = w2_hi[:].rearrange("p (c d) -> p c d", c=FC)
        w2l = w2_lo[:].rearrange("p (c d) -> p c d", c=FC)
        scan_a = exp_k
        scan_b = k_rest[:].rearrange("p c (j t) -> p c j t", j=PAIR)
        mix = q_all[:].rearrange("p c (j t) -> p c j t", j=PAIR)
        mix_a = k_all[:].rearrange("p c (j t) -> p c j t", j=PAIR)

        up_ps = [ctx.enter_context(nc.psum_tensor(f"up_ps{i}", [P, TOK], F32)) for i in range(2)]
        down_ps = [ctx.enter_context(nc.psum_tensor(f"down_ps{i}", [P, 512], F32)) for i in range(2)]
        bank = [ctx.enter_context(nc.psum_tensor(f"bank{i}", [P, 512], F32)) for i in range(4)]

        def by_chunk(t):
            return t[:].rearrange("p (c n) -> p c n", c=C)

        def by_head(t):
            return t[:].rearrange("p (h t) -> p h t", h=HQ)

        def by_tile(t):
            return t[:].rearrange("p (j d) -> p j d", j=PAIR)

        def by_cjt(t):
            return t[:].rearrange("p (c j t) -> p c j t", c=C, j=PAIR)

        consts_loaded = sem("consts_loaded")
        masks_made = sem("masks_made")
        proj_loaded = sem("proj_loaded")
        proj_hi_ready = sem("proj_hi_ready")
        proj_ready = sem("proj_ready")
        decay_ready = sem("decay_ready")
        dve_setup = sem("dve_setup")
        act_setup = sem("act_setup")
        x_loaded = sem("x_loaded")
        ctx_loaded = sem("ctx_loaded")
        xt_ps = sem("xt_ps")
        xt_hi_ready = sem("xt_hi_ready")
        xt_ready = sem("xt_ready")
        q_ps = sem("q_ps")
        k_ps = sem("k_ps")
        v_ps = sem("v_ps")
        q_hi_ready = sem("q_hi_ready")
        q_ready = sem("q_ready")
        k_hi_ready = sem("k_hi_ready")
        k_rest_ready = sem("k_rest_ready")
        kd_ready = sem("kd_ready")
        v_step = sem("v_step")
        scores_ps = sem("scores_ps")
        max_ready = sem("max_ready")
        shifted = sem("shifted")
        probs_ready = sem("probs_ready")
        pt_ps = sem("pt_ps")
        pt_hi_ready = sem("pt_hi_ready")
        pt_ready = sem("pt_ready")
        pv_ps = sem("pv_ps")
        inv_ready = sem("inv_ready")
        att_ready = sem("att_ready")
        att_t_ps = sem("att_t_ps")
        att_hi_ready = sem("att_hi_ready")
        att_t_ready = sem("att_t_ready")
        wo_ps = sem("wo_ps")
        x_bo_ready = sem("x_bo_ready")
        y1_sum = sem("y1_sum")
        ln1_step = sem("ln1_step")
        ln1_eps = sem("ln1_eps")
        ln1_rstd = sem("ln1_rstd")
        y1_ready = sem("y1_ready")
        ctx_t_ps = sem("ctx_t_ps")
        ctx_t_ready = sem("ctx_t_ready")
        y1t_ps = sem("y1t_ps")
        exps_ready = sem("exps_ready")
        xa_step = sem("xa_step")
        mix_a_ready = sem("mix_a_ready")
        mix_ready = sem("mix_ready")
        x2_ps = sem("x2_ps")
        ln2_step = sem("ln2_step")
        ln2_eps = sem("ln2_eps")
        ln2_rstd = sem("ln2_rstd")
        x2_ready = sem("x2_ready")
        x2t_ps = sem("x2t_ps")
        x2t_hi_ready = sem("x2t_hi_ready")
        x2t_ready = sem("x2t_ready")
        logits_t_ps = sem("logits_t_ps")
        logits_t_ready = sem("logits_t_ready")
        logits_ps = sem("logits_ps")
        route_step = sem("route_step")
        route_exp = sem("route_exp")
        gate_ready = sem("gate_ready")
        gate_t_ps = sem("gate_t_ps")
        gate_hi_ready = sem("gate_hi_ready")
        gate_t_ready = sem("gate_t_ready")
        b2_ps = sem("b2_ps")
        acc_ready = sem("acc_ready")
        ln3_step = sem("ln3_step")
        ln3_eps = sem("ln3_eps")
        ln3_rstd = sem("ln3_rstd")
        out_ready = sem("out_ready")
        stored = sem("stored")
        w1_loaded = sem("w1_loaded")
        w2_loaded = sem("w2_loaded")
        w1_hi_ready = sem("w1_hi_ready")
        w1_ready = sem("w1_ready")
        w2_hi_ready = sem("w2_hi_ready")
        w2_ready = sem("w2_ready")
        up_done = sem("up_done")
        gelu_done = sem("gelu_done")
        h_hi_ready = sem("h_hi_ready")
        h_ready = sem("h_ready")
        down_done = sem("down_done")
        added = sem("added")

        CONSTS = 8
        block = ctx.enter_context(nc.Block())


        @block.sync
        def _(sp):
            def load_pair(p):
                sp.wait_ge(y1_sum, p)
                sp.dma_start(x_in[:], x[bass.ds(PAIR * p, PAIR)].rearrange("j s d -> s j d")).then_inc(x_loaded, 16)
                sp.wait_ge(ctx_t_ps, p)
                sp.dma_start(ctx_sb[:], ctx_in[bass.ds(PAIR * p, PAIR)].rearrange("j s d -> s j d")).then_inc(ctx_loaded, 16)

            def load_w1(e, n):
                sp.wait_ge(w1_ready, PIECES * n)
                sp.dma_start(w1_raw[:].rearrange("p (c f) -> p c f", c=C),
                             w1[bass.ds(e, 1)].rearrange("a (c p) f -> p (a c) f", p=P)).then_inc(w1_loaded, 16)

            def load_w2(e, n):
                sp.wait_ge(w2_ready, PIECES * n)
                sp.dma_start(w2_raw[:].rearrange("p (c d) -> p c d", c=FC),
                             w2[bass.ds(e, 1)].rearrange("a (c p) d -> p (a c) d", p=P)).then_inc(w2_loaded, 16)

            def store(b):
                sp.wait_ge(out_ready, b + 1)
                sp.dma_start(out[bass.ds(BLK * b, BLK)].rearrange("j s d -> s j d"), acc[:]).then_inc(stored, 16)

            sp.dma_start(x_in[:], x[0:PAIR].rearrange("j s d -> s j d")).then_inc(x_loaded, 16)
            for i, w in enumerate((wq, wk, wv, wo)):
                sp.dma_start(w2_raw[:].rearrange("p (i c d) -> p i c d", i=4, c=C)[:, i],
                             w.rearrange("(c p) d -> p c d", p=P)).then_inc(proj_loaded, 16)
            sp.dma_start(bqk[:], cols[:, 0:2, :]).then_inc(consts_loaded, 16)
            sp.dma_start(wu[:], cols[:, 2:4, :]).then_inc(consts_loaded, 16)
            sp.dma_start(bv_all[:], bv.rearrange("(a d) -> a d", a=1).to_broadcast([P, D])).then_inc(consts_loaded, 16)
            sp.dma_start(bo_all[:], bo.rearrange("(a d) -> a d", a=1).to_broadcast([P, D])).then_inc(consts_loaded, 16)
            for c in range(C):
                sp.dma_start(wg_raw[:, c, :], wg[c]).then_inc(consts_loaded, 16)
            sp.dma_start(b1_all[:], b1).then_inc(consts_loaded, 16)
            sp.dma_start(b2_raw[:], b2).then_inc(consts_loaded, 16)
            sp.dma_start(ctx_sb[:], ctx_in[0:PAIR].rearrange("j s d -> s j d")).then_inc(ctx_loaded, 16)
            load_w1(0, 0)
            sp.wait_ge(proj_ready, PIECES)
            load_w2(0, 0)
            load_pair(1)

            with sp.Fori(0, NBLK - 1) as b:
                with sp.Fori(0, E // SC) as half:
                    load_pair(2 * b + half + 2)
                    for k in range(SC):
                        after = half * SC + (k + 1) if k < SC - 1 else half * -SC + SC
                        load_w1(after, b * E + half * SC + (k + 1))
                        load_w2(after, b * E + half * SC + (k + 1))
                store(b)
            with sp.Fori(0, E - 1) as e:
                load_w1(e + 1, e + ((NBLK - 1) * E + 1))
                load_w2(e + 1, e + ((NBLK - 1) * E + 1))
            store(NBLK - 1)
            sp.wait_ge(stored, 16 * NBLK)

        @block.tensor
        def _(pe):
            def product(ps, hi, lo, rhs_hi, rhs_lo, first=True, last=True):
                nc.tensor.matmul(ps, hi, rhs_hi, start=first, stop=False)
                nc.tensor.matmul(ps, hi, rhs_lo, start=False, stop=False)
                return nc.tensor.matmul(ps, lo, rhs_hi, start=False, stop=last)

            def project(ps, which, c):
                for kc in range(C):
                    cols = slice(c * P, (c + 1) * P)
                    mm = product(ps, proj_hi[:, which, kc, cols], proj_lo[:, which, kc, cols],
                                 xt_hi[:, kc, :], xt_lo[:, kc, :], kc == 0, kc == C - 1)
                return mm

            def project_rows(ps, which, j):
                for kc in range(C):
                    rows = slice(j * S, (j + 1) * S)
                    mm = product(ps, xt_hi[:, kc, rows], xt_lo[:, kc, rows],
                                 proj_hi[:, which, kc, :], proj_lo[:, which, kc, :], kc == 0, kc == C - 1)
                return mm

            def turn(dst, src):
                for c in range(C):
                    for j in range(PAIR):
                        mm = nc.tensor.transpose(dst[:, c, j * S:(j + 1) * S], src[:, j, c * P:(c + 1) * P], ident[:])
                return mm

            def scores(p, u):
                c, j = divmod(u, PAIR)
                if j == 0:
                    pe.wait_ge(kd_ready, C * p + (c + 1))
                rows = slice(j * S, (j + 1) * S)
                if u == 2:
                    pe.wait_ge(att_ready, UNITS * p + 2)
                for i in range(2):
                    if u % 2:
                        pe.wait_ge(shifted, QUADS * p + (2 * u - 1 + i))
                    heads = slice(i * HQ, (i + 1) * HQ)
                    product(by_head(bank[i]), q_hi[:, c, rows], q_lo[:, c, rows],
                            kd_hi[:, j, heads, :], kd_lo[:, j, heads, :]).then_inc(scores_ps, 1)

            def turn_probs(p, u):
                for i in range(2):
                    g = 2 * u + i
                    pe.wait_ge(probs_ready, QUADS * p + (g + 1))
                    for h in range(HQ):
                        mm = nc.tensor.transpose(by_head(bank[2 + i])[:, h, :], probs[:, u % 2, i, h, :], ident[:])
                    mm.then_inc(pt_ps, 1)

            def weigh_values(p, u):
                c, j = divmod(u, PAIR)
                if u == 0:
                    pe.wait_ge(v_step, 5 * (p + 1))
                if u % 2 == 0:
                    pe.wait_ge(shifted, QUADS * p + (2 * u + 4))
                for i in range(2):
                    pe.wait_ge(pt_ready, QUADS * p + (2 * u + i + 1))
                    for h in range(HQ):
                        slot = i * HQ + h
                        ps = bank[u % 2][:, slot * VW:(slot + 1) * VW]
                        head = c * HC + i * HQ + h
                        hi, lo = pt_hi[:, i, h, :], pt_lo[:, i, h, :]
                        nc.tensor.matmul(ps, hi, v_hi[:, j, head, :], start=True, stop=False)
                        nc.tensor.matmul(ps, hi, v_mid[:, j, head, :], start=False, stop=False)
                        nc.tensor.matmul(ps, hi, v_lo[:, j, head, :], start=False, stop=False)
                        nc.tensor.matmul(ps, lo, v_hi[:, j, head, :], start=False, stop=False)
                        mm = nc.tensor.matmul(ps, lo, v_mid[:, j, head, :], start=False, stop=True)
                    mm.then_inc(pv_ps, 1)

            def attend(p, s):
                if s == X_STEP:
                    pe.wait_ge(x_loaded, 16 * (p + 1))
                    turn(by_chunk(bank[0]), x_in).then_inc(xt_ps, 1)
                if s == QK_STEP:
                    pe.wait_ge(xt_ready, p + 1)
                    project(by_chunk(bank[1])[:, 0, :], 0, 0)
                    project(by_chunk(bank[1])[:, 1, :], 0, 1).then_inc(q_ps, 1)
                    project(by_chunk(bank[2])[:, 0, :], 1, 0)
                    project(by_chunk(bank[2])[:, 1, :], 1, 1).then_inc(k_ps, 1)
                if s == V_STEP:
                    project_rows(by_tile(bank[3])[:, 0, :], 2, 0)
                    project_rows(by_tile(bank[3])[:, 1, :], 2, 1).then_inc(v_ps, 1)
                if s == SCORE_STEP[0]:
                    pe.wait_ge(q_ready, p + 1)
                for u in range(UNITS):
                    if s == SCORE_STEP[u]:
                        scores(p, u)
                    if s == TURN_STEP[u]:
                        turn_probs(p, u)
                    if s == VALUE_STEP[u]:
                        weigh_values(p, u)
                if s == ATT_STEP:
                    pe.wait_ge(att_ready, UNITS * (p + 1))
                    turn(by_chunk(bank[2]), att).then_inc(att_t_ps, 1)
                if s == WO_STEP:
                    pe.wait_ge(att_t_ready, p + 1)
                    project_rows(by_tile(bank[3])[:, 0, :], 3, 0)
                    project_rows(by_tile(bank[3])[:, 1, :], 3, 1).then_inc(wo_ps, 1)
                if s == CTX_STEP:
                    pe.wait_ge(ctx_loaded, 16 * (p + 1))
                    turn(by_chunk(bank[1]), ctx_sb).then_inc(ctx_t_ps, 1)
                if s == Y1_STEP:
                    pe.wait_ge(y1_ready, p + 1)
                    turn(by_chunk(bank[0]), y1).then_inc(y1t_ps, 1)
                if s == BACK_STEP:
                    pe.wait_ge(mix_ready, p + 1)
                    for j in range(PAIR):
                        for c in range(C):
                            mm = nc.tensor.transpose(by_tile(bank[2])[:, j, c * P:(c + 1) * P], mix[:, c, j, :], ident[:])
                    mm.then_inc(x2_ps, 1)

            def route(b):
                pe.wait_ge(x2_ready, 2 * (b + 1))
                for c in range(C):
                    for t in range(BLK):
                        mm = nc.tensor.transpose(bank[c][:, t * S:(t + 1) * S], x2[:, t, c * P:(c + 1) * P], ident[:])
                    mm.then_inc(x2t_ps, 1)
                pe.wait_ge(x2t_ready, C * (b + 1))
                for kc in range(C):
                    mm = product(bank[2][:], wg_hi[:, kc, :], wg_lo[:, kc, :],
                                 x2t_hi[:, kc, :], x2t_lo[:, kc, :], kc == 0, kc == C - 1)
                mm.then_inc(logits_t_ps, 1)
                pe.wait_ge(logits_t_ready, b + 1)
                for t in range(BLK):
                    mm = nc.tensor.transpose(bank[3][:, t * P:(t + 1) * P], logits_t[:, t * S:(t + 1) * S], ident[:])
                mm.then_inc(logits_ps, 1)
                pe.wait_ge(gate_ready, b + 1)
                for t in range(BLK):
                    mm = nc.tensor.transpose(bank[2][0:E, t * S:(t + 1) * S], gate[:, t, :], ident[:])
                mm.then_inc(gate_t_ps, 1)
                pe.wait_ge(gate_t_ready, b + 1)
                for t in range(BLK):
                    rows = slice(t * S, (t + 1) * S)
                    mm = product(by_tile(bank[t // 2])[:, t % 2, :], gt_hi[:, rows], gt_lo[:, rows], b2_hi[:], b2_lo[:])
                mm.then_inc(b2_ps, 1)

            def up(n, c):
                if c == 0:
                    pe.wait_ge(w1_ready, PIECES * (n + 1))
                if c >= 2:
                    pe.wait_ge(gelu_done, FC * n + (c - 1))
                cols = slice(c * P, (c + 1) * P)
                for kc in range(C):
                    mm = product(up_ps[c % 2][:], w1h[:, kc, cols], w1l[:, kc, cols],
                                 x2t_hi[:, kc, :], x2t_lo[:, kc, :], kc == 0, kc == C - 1)
                mm.then_inc(up_done, 1)

            def down(n, t):
                if t == 0:
                    pe.wait_ge(w2_ready, PIECES * (n + 1))
                if t >= 2:
                    pe.wait_ge(added, BLK * n + (t - 1))
                rows = slice(t * S, (t + 1) * S)
                for c in range(FC):
                    if t == 0:
                        pe.wait_ge(h_ready, FC * n + (c + 1))
                    mm = product(down_ps[t % 2][:, 0:D], h_hi[:, c, rows], h_lo[:, c, rows],
                                 w2h[:, c, :], w2l[:, c, :], c == 0, c == FC - 1)
                mm.then_inc(down_done, 1)

            pe.wait_ge(masks_made, MASKS)
            pe.wait_ge(proj_ready, PIECES)
            pe.wait_ge(dve_setup, DVE_SETUP)
            with pe.Fori(0, 2) as p:
                for s in range(STEPS):
                    attend(p, s)
            route(0)
            with pe.Fori(0, NBLK - 1) as b:
                with pe.Fori(0, E // SC) as half:
                    for k in range(SC):
                        for c in range(FC):
                            up(b * E + half * SC + k, c)
                            if k == 0 and c == 0:
                                pe.wait_ge(acc_ready, b + 1)
                            attend(2 * b + half + 2, k * SLOTS + c)
                        for t in range(BLK):
                            down(b * E + half * SC + k, t)
                            attend(2 * b + half + 2, k * SLOTS + FC + t)
                route(b + 1)
            with pe.Fori(0, E) as e:
                for c in range(FC):
                    up(e + (NBLK - 1) * E, c)
                for t in range(BLK):
                    down(e + (NBLK - 1) * E, t)

        @block.scalar
        def _(act):
            def split_hi(dst, src, i):
                cols = slice(i * PW, (i + 1) * PW)
                return nc.scalar.activation(dst[:, cols], src[:, cols], ACT.Copy)

            def attend(p, s):
                if s == X_STEP:
                    act.wait_ge(xt_ps, p + 1)
                    nc.scalar.activation(xt_hi[:], by_chunk(bank[0]), ACT.Copy).then_inc(xt_hi_ready, 1)
                if s == QK_STEP:
                    act.wait_ge(q_ps, p + 1)
                    for dst in (q_all, q_hi):
                        for c in range(C):
                            a = nc.scalar.activation(dst[:, c, :], by_chunk(bank[1])[:, c, :], ACT.Identity,
                                                     bias=bq_scaled[:, c:c + 1], scale=DH ** -0.5)
                    a.then_inc(q_hi_ready, 1)
                    act.wait_ge(k_ps, p + 1)
                    for dst in (k_all, k_hi):
                        for c in range(C):
                            a = nc.scalar.activation(dst[:, c, :], by_chunk(bank[2])[:, c, :], ACT.Identity,
                                                     bias=bqk[:, 1, c:c + 1])
                    a.then_inc(k_hi_ready, 1)
                for u in range(UNITS):
                    if s == EXP_STEP[u]:
                        for i in range(2):
                            act.wait_ge(shifted, QUADS * p + (2 * u + i + 1))
                            nc.scalar.activation(probs[:, u % 2, i], probs[:, u % 2, i], ACT.Exp).then_inc(probs_ready, 1)
                    if s == TURN_STEP[u]:
                        for i in range(2):
                            g = 2 * u + i
                            act.wait_ge(pt_ps, QUADS * p + (g + 1))
                            if u > 0:
                                act.wait_ge(pv_ps, QUADS * p + (g - 1))
                            nc.scalar.activation(pt_hi[:, i], by_head(bank[2 + i]), ACT.Copy).then_inc(pt_hi_ready, 1)
                if s == ATT_STEP:
                    act.wait_ge(att_t_ps, p + 1)
                    nc.scalar.activation(xt_hi[:], by_chunk(bank[2]), ACT.Copy).then_inc(att_hi_ready, 1)
                if s == CTX_STEP:
                    act.wait_ge(ctx_t_ps, p + 1)
                    nc.scalar.activation(ctx_t[:], by_cjt(bank[1]), ACT.Copy).then_inc(ctx_t_ready, 1)
                if s == XEXP_STEP:
                    act.wait_ge(y1t_ps, p + 1)
                    k = by_cjt(bank[0])
                    nc.scalar.activation(y1t[:], k, ACT.Copy)
                    nc.scalar.activation(exp_k[:], k, ACT.Exp)
                    nc.scalar.activation(inc_b[:, :, :, 2:S], k[:, :, :, 1:S - 1], ACT.Exp, scale=-1.0)
                    for c in range(C):
                        a = nc.scalar.activation(exp_uk[:, c], k[:, c], ACT.Exp, bias=wu[:, 1, c:c + 1])
                    a.then_inc(exps_ready, 1)

            def route(b):
                for c in range(C):
                    act.wait_ge(x2t_ps, C * b + (c + 1))
                    nc.scalar.activation(x2t_hi[:, c, :], bank[c][:], ACT.Copy).then_inc(x2t_hi_ready, 1)
                act.wait_ge(logits_t_ps, b + 1)
                nc.scalar.activation(logits_t[:], bank[2][:], ACT.Copy).then_inc(logits_t_ready, 1)
                act.wait_ge(route_step, 4 * b + 2)
                nc.scalar.activation(route_exps[:], logits[:], ACT.Exp).then_inc(route_exp, 1)
                act.wait_ge(gate_t_ps, b + 1)
                nc.scalar.activation(gt_hi[:], bank[2][0:E, :], ACT.Copy).then_inc(gate_hi_ready, 1)

            def hidden_hi(n, c):
                act.wait_ge(gelu_done, FC * n + (c + 1))
                nc.scalar.activation(h_hi[:, c, :], h_all[:, c % 2, :], ACT.Copy).then_inc(h_hi_ready, 1)

            def hidden(n, e, c):
                act.wait_ge(up_done, FC * n + (c + 1))
                if c >= 2:
                    act.wait_ge(h_ready, FC * n + (c - 1))
                nc.scalar.activation(h_all[:, c % 2, :], up_ps[c % 2][:], ACT.Gelu_apprx_tanh,
                                     bias=b1_all[:, bass.ds(e * FC + c, 1)]).then_inc(gelu_done, 1)
                if c > 0:
                    hidden_hi(n, c - 1)
                if c < PIECES:
                    if c == 0:
                        act.wait_ge(w2_loaded, 16 * (n + 1))
                    split_hi(w2_hi, w2_raw, c).then_inc(w2_hi_ready, 1)
                if c == FC - 1:
                    hidden_hi(n, c)

            def split_w1(n, i):
                if i == 0:
                    act.wait_ge(w1_loaded, 16 * (n + 1))
                    if not isinstance(n, int):
                        act.wait_ge(up_done, FC * n)
                split_hi(w1_hi, w1_raw, i).then_inc(w1_hi_ready, 1)

            act.wait_ge(consts_loaded, 16 * CONSTS)
            nc.scalar.activation(decay[:, 0, :], wu[:, 0, :], ACT.Exp, scale=-1.0)
            nc.scalar.activation(decay[:, 1, :], wu[:, 0, :], ACT.Exp).then_inc(decay_ready, 1)
            nc.scalar.activation(bq_scaled[:], bqk[:, 0, :], ACT.Copy, scale=DH ** -0.5).then_inc(act_setup, 1)
            nc.scalar.activation(b2_hi[:], b2_raw[:], ACT.Copy).then_inc(act_setup, 1)
            act.wait_ge(dve_setup, 1)
            nc.scalar.activation(wg_hi[:, :, 0:E], wg_raw[:], ACT.Copy).then_inc(act_setup, 1)
            act.wait_ge(proj_loaded, 16 * 4)
            for i in range(4):
                nc.scalar.activation(proj_hi[:, i], w2_raw[:].rearrange("p (i c d) -> p i c d", i=4, c=C)[:, i],
                                     ACT.Copy).then_inc(proj_hi_ready, 1)
            for i in range(PIECES):
                split_w1(0, i)
            act.wait_ge(act_setup, 3)
            with act.Fori(0, 2) as p:
                for s in range(STEPS):
                    attend(p, s)
            route(0)
            with act.Fori(0, NBLK - 1) as b:
                with act.Fori(0, E // SC) as half:
                    for k in range(SC):
                        n = b * E + half * SC + k
                        for c in range(FC):
                            hidden(n, half * SC + k, c)
                            attend(2 * b + half + 2, k * SLOTS + c)
                        for t in range(BLK):
                            split_w1(b * E + half * SC + (k + 1), t)
                            attend(2 * b + half + 2, k * SLOTS + FC + t)
                route(b + 1)
            with act.Fori(0, E - 1) as e:
                for c in range(FC):
                    hidden(e + (NBLK - 1) * E, e, c)
                for i in range(PIECES):
                    split_w1(e + ((NBLK - 1) * E + 1), i)
            for c in range(FC):
                hidden(NBLK * E - 1, E - 1, c)

        @block.vector
        def _(dve):
            def low(dst, src, hi):
                return nc.vector.tensor_tensor(dst, src, hi.bitcast(F32), ALU.subtract)

            def norm(src, dst, which, tiles, step, eps_done, base, summed=None):
                for j in range(tiles):
                    i = nc.vector.bn_stats(stats[:, j, :], src[j])
                i.then_inc(step, 1)
                dve.wait_ge(step, 2 * base + 1)
                nc.vector.tensor_copy(spare[:, which:which + 1], stats[:, 0, 1:2])
                for j in range(tiles):
                    i = nc.vector.bn_aggr(moments[:, which, j, :], stats[:, j, :])
                i.then_inc(step, 1)
                dve.wait_ge(step, 2 * base + 2)
                dve.wait_ge(eps_done, base + 1)
                for j in range(tiles):
                    i = nc.vector.tensor_scalar(dst[j], src[j], moments[:, which, j, 0:1], rstd[:, which, j:j + 1],
                                                ALU.subtract, ALU.mult)
                return i

            def diagonal(p, c):
                if c > 0:
                    dve.wait_ge(scores_ps, QUADS * p + 2 * PAIR * c)
                for dst, src in ((kd_hi, k_all), (kd_lo, k_rest)):
                    for h in range(HC):
                        i = nc.vector.tensor_scalar(dst[:, :, h, :], src[:, c, :].rearrange("p (j t) -> p j t", j=PAIR),
                                                    head_mask[:, h:h + 1], None, ALU.mult)
                i.then_inc(kd_ready, 1)

            def attend(p, s):
                if s == X_STEP:
                    dve.wait_ge(xt_hi_ready, p + 1)
                    low(xt_lo[:], by_chunk(bank[0]), xt_hi[:]).then_inc(xt_ready, 1)
                if s == QK_STEP:
                    dve.wait_ge(q_hi_ready, p + 1)
                    low(q_lo[:], q_all[:], q_hi[:]).then_inc(q_ready, 1)
                    dve.wait_ge(k_hi_ready, p + 1)
                    low(k_rest[:], k_all[:], k_hi[:]).then_inc(k_rest_ready, 1)
                    dve.wait_ge(k_rest_ready, p + 1)
                    diagonal(p, 0)
                if s == V_STEP:
                    def heads(t):
                        return t[:].rearrange("p j (h e) -> p j h e", h=H)

                    dve.wait_ge(v_ps, p + 1)
                    for j in range(PAIR):
                        i = nc.vector.tensor_tensor(v_all[:, j], by_tile(bank[3])[:, j], bv_all[:], ALU.add)
                    i.then_inc(v_step, 1)
                    dve.wait_ge(v_step, 5 * p + 1)
                    nc.vector.tensor_copy(v_hi[:, :, :, 0:DH], heads(v_all)).then_inc(v_step, 1)
                    dve.wait_ge(v_step, 5 * p + 2)
                    nc.vector.tensor_tensor(heads(v_all), heads(v_all), v_hi[:, :, :, 0:DH], ALU.subtract).then_inc(v_step, 1)
                    dve.wait_ge(v_step, 5 * p + 3)
                    nc.vector.tensor_copy(v_mid[:, :, :, 0:DH], heads(v_all)).then_inc(v_step, 1)
                    dve.wait_ge(v_step, 5 * p + 4)
                    nc.vector.tensor_tensor(v_lo[:, :, :, 0:DH], heads(v_all), v_mid[:, :, :, 0:DH], ALU.subtract).then_inc(v_step, 1)
                for u in range(UNITS):
                    c, j = divmod(u, PAIR)
                    if s == SCORE_STEP[u]:
                        for i in range(2):
                            g = 2 * u + i
                            dve.wait_ge(scores_ps, QUADS * p + (g + 1))
                            nc.vector.tensor_reduce(neg_max[:, g, :], by_head(bank[i]), AX_X, ALU.max,
                                                    negate=True).then_inc(max_ready, 1)
                        for i in range(2):
                            g = 2 * u + i
                            dve.wait_ge(max_ready, QUADS * p + (g + 1))
                            if u >= 2:
                                dve.wait_ge(pt_ps, QUADS * p + (g - 3))
                            nc.vector.tensor_tensor(probs[:, u % 2, i], by_head(bank[i]),
                                                    neg_max[:, g, :].rearrange("p (h a) -> p h a", a=1).to_broadcast([P, HQ, S]),
                                                    ALU.add).then_inc(shifted, 1)
                    if s == SCORE_STEP[u] + 1 and u == PAIR - 1:
                        diagonal(p, 1)
                    if s == TURN_STEP[u]:
                        for i in range(2):
                            g = 2 * u + i
                            dve.wait_ge(pt_hi_ready, QUADS * p + (g + 1))
                            nc.vector.tensor_tensor(pt_lo[:, i], by_head(bank[2 + i]), pt_hi[:, i], ALU.subtract)\
                                .then_inc(pt_ready, 1)
                    if s == VALUE_STEP[u]:
                        dve.wait_ge(pv_ps, QUADS * p + (2 * u + 2))
                        rows = bank[u % 2][:, 0:HC * VW].rearrange("p (h e) -> p h e", h=HC)
                        nc.vector.reciprocal(inv_sum[:, u, :], rows[:, :, DH]).then_inc(inv_ready, 1)
                        dve.wait_ge(inv_ready, UNITS * p + (u + 1))
                        nc.vector.tensor_tensor(att[:, j, c * P:(c + 1) * P].rearrange("p (h e) -> p h e", h=HC), rows[:, :, 0:DH],
                                                inv_sum[:, u, :].rearrange("p (h a) -> p h a", a=1).to_broadcast([P, HC, DH]),
                                                ALU.mult).then_inc(att_ready, 1)
                if s == ATT_STEP:
                    dve.wait_ge(att_hi_ready, p + 1)
                    low(xt_lo[:], by_chunk(bank[2]), xt_hi[:]).then_inc(att_t_ready, 1)
                if s == WO_STEP:
                    dve.wait_ge(wo_ps, p + 1)
                    dve.wait_ge(x_bo_ready, p + 1)
                    nc.vector.tensor_tensor(y1[:], by_tile(bank[3]), x_bo[:], ALU.add).then_inc(y1_sum, 1)
                    dve.wait_ge(y1_sum, p + 1)
                    tiles = [y1[:, j] for j in range(PAIR)]
                    norm(tiles, tiles, 0, PAIR, ln1_step, ln1_rstd, p).then_inc(y1_ready, 1)
                if s == REC_STEP:
                    dve.wait_ge(exps_ready, p + 1)
                    dve.wait_ge(ctx_t_ready, p + 1)
                    nc.vector.tensor_tensor(inc_a[:, :, :, 2:S], exp_k[:, :, :, 1:S - 1], ctx_t[:, :, :, 1:S - 1],
                                            ALU.mult).then_inc(xa_step, 1)
                    dve.wait_ge(xa_step, 6 * p + 1)
                    for i, (state, inc) in enumerate(((scan_a, inc_a), (scan_b, inc_b))):
                        for c in range(C):
                            for j in range(PAIR):
                                o = nc.vector.tensor_tensor_scan(state[:, c, j, :], decay_row[:, i, c, :], inc[:, c, j, :],
                                                                 0.0, ALU.mult, ALU.add)
                        o.then_inc(xa_step, 1)
                    flat = mix.rearrange("p c j t -> p (c j) t")
                    dve.wait_ge(xa_step, 6 * p + 3)
                    nc.vector.tensor_tensor(mix, ctx_t[:], scan_b, ALU.mult).then_inc(xa_step, 1)
                    dve.wait_ge(xa_step, 6 * p + 4)
                    nc.vector.tensor_tensor(flat, flat, ramp[:].rearrange("p (a t) -> p a t", a=1).to_broadcast([P, C * PAIR, S]),
                                            ALU.add).then_inc(xa_step, 1)
                    dve.wait_ge(xa_step, 6 * p + 5)
                    nc.vector.tensor_tensor(mix, mix, exp_uk[:], ALU.mult).then_inc(xa_step, 1)
                    dve.wait_ge(xa_step, 6 * p + 6)
                    dve.wait_ge(mix_a_ready, p + 1)
                    nc.vector.tensor_tensor(mix, mix, mix_a, ALU.add).then_inc(mix_ready, 1)
                if s == BACK_STEP:
                    dve.wait_ge(x2_ps, p + 1)
                    norm([by_tile(bank[2])[:, j] for j in range(PAIR)], x2_tiles(p), 1, PAIR, ln2_step, ln2_rstd, p)\
                        .then_inc(x2_ready, 1)

            half_of = {}

            def x2_tiles(p):
                return [x2[:, bass.ds(PAIR * half_of["pair"] + j, 1), :].rearrange("p a d -> p (a d)") for j in range(PAIR)]

            def route(b):
                for c in range(C):
                    dve.wait_ge(x2t_hi_ready, C * b + (c + 1))
                    low(x2t_lo[:, c, :], bank[c][:], x2t_hi[:, c, :]).then_inc(x2t_ready, 1)
                dve.wait_ge(logits_ps, b + 1)
                lg = bank[3][:].rearrange("p (t e) -> p t e", t=BLK)[:, :, 0:E]

                def over_experts(v):
                    return v[:].rearrange("p (t a) -> p t a", a=1).to_broadcast([P, BLK, E])

                nc.vector.tensor_reduce(route_max[:], lg, AX_X, ALU.max, negate=True).then_inc(route_step, 1)
                dve.wait_ge(route_step, 4 * b + 1)
                nc.vector.tensor_tensor(logits[:], lg, over_experts(route_max), ALU.add).then_inc(route_step, 1)
                dve.wait_ge(route_exp, b + 1)
                nc.vector.tensor_reduce(route_sum[:], route_exps[:], AX_X, ALU.add).then_inc(route_step, 1)
                dve.wait_ge(route_step, 4 * b + 3)
                nc.vector.reciprocal(route_inv[:], route_sum[:]).then_inc(route_step, 1)
                dve.wait_ge(route_step, 4 * b + 4)
                nc.vector.tensor_tensor(gate[:], route_exps[:], over_experts(route_inv), ALU.mult).then_inc(gate_ready, 1)
                dve.wait_ge(gate_hi_ready, b + 1)
                low(gt_lo[:], bank[2][0:E, :], gt_hi[:]).then_inc(gate_t_ready, 1)
                dve.wait_ge(b2_ps, b + 1)
                dve.wait_ge(stored, 16 * b)
                for i in range(2):
                    o = nc.vector.tensor_tensor(acc[:, 2 * i:2 * i + 2, :], by_tile(bank[i]), x2[:, 2 * i:2 * i + 2, :], ALU.add)
                o.then_inc(acc_ready, 1)

            def hidden_lo(n, c):
                dve.wait_ge(h_hi_ready, FC * n + (c + 1))
                low(h_lo[:, c, :], h_all[:, c % 2, :], h_hi[:, c, :]).then_inc(h_ready, 1)

            def add_expert(n, e, t):
                dve.wait_ge(down_done, BLK * n + (t + 1))
                nc.vector.scalar_tensor_tensor(out=acc[:, t, :], in0=down_ps[t % 2][:, 0:D],
                                               scalar=gate[:, t, bass.ds(e, 1)], in1=acc[:, t, :],
                                               op0=ALU.mult, op1=ALU.add).then_inc(added, 1)

            def expert_up(n, c):
                if c > 0:
                    hidden_lo(n, c - 1)
                if c == FC - 1:
                    hidden_lo(n, c)

            def finish(b):
                dve.wait_ge(added, BLK * E * (b + 1))
                tiles = [acc[:, t] for t in range(BLK)]
                norm(tiles, tiles, 2, BLK, ln3_step, ln3_rstd, b).then_inc(out_ready, 1)

            nc.vector.memset(wg_hi[:].bitcast(F32), 0.0)
            nc.vector.memset(wg_lo[:].bitcast(F32), 0.0).then_inc(dve_setup, 1)
            nc.vector.memset(inc_a[:, :, :, 0:2], 0.0)
            nc.vector.memset(inc_b[:, :, :, 0:2], 0.0)
            nc.vector.memset(v_hi[:, :, :, DH:VW], 1.0)
            nc.vector.memset(v_mid[:, :, :, DH:VW], 0.0)
            nc.vector.memset(v_lo[:, :, :, DH:VW], 0.0)
            nc.vector.memset(ones[:], 1.0).then_inc(dve_setup, 1)
            dve.wait_ge(dve_setup, 2)
            nc.vector.tensor_tensor_scan(ramp[:], ones[:], ones[:], 0.0, ALU.mult, ALU.add).then_inc(dve_setup, 1)
            dve.wait_ge(dve_setup, 3)
            nc.vector.tensor_scalar(ramp[:], ramp[:], -2.0, 0.0, ALU.add, ALU.max)
            dve.wait_ge(decay_ready, 1)
            for i in range(2):
                for c in range(C):
                    nc.vector.tensor_scalar(decay_row[:, i, c, :], ones[:], decay[:, i, c:c + 1], None, ALU.mult)
            dve.wait_ge(act_setup, 3)
            low(wg_lo[:, :, 0:E], wg_raw[:], wg_hi[:, :, 0:E])
            low(b2_lo[:], b2_raw[:], b2_hi[:]).then_inc(dve_setup, 1)
            for i in range(PIECES):
                dve.wait_ge(proj_hi_ready, i + 1)
                low(proj_lo[:, i], w2_raw[:].rearrange("p (i c d) -> p i c d", i=4, c=C)[:, i], proj_hi[:, i])\
                    .then_inc(proj_ready, 1)
            dve.wait_ge(masks_made, MASKS)
            dve.wait_ge(dve_setup, DVE_SETUP)
            with dve.Fori(0, 2) as p:
                half_of["pair"] = p
                for s in range(STEPS):
                    attend(p, s)
            route(0)
            with dve.Fori(0, NBLK - 1) as b:
                with dve.Fori(0, E // SC) as half:
                    half_of["pair"] = half
                    for k in range(SC):
                        n = b * E + half * SC + k
                        for c in range(FC):
                            expert_up(n, c)
                            attend(2 * b + half + 2, k * SLOTS + c)
                        for t in range(BLK):
                            if k == 0 and t == 0:
                                dve.wait_ge(acc_ready, b + 1)
                            add_expert(n, half * SC + k, t)
                            attend(2 * b + half + 2, k * SLOTS + FC + t)
                finish(b)
                route(b + 1)
            with dve.Fori(0, E) as e:
                for c in range(FC):
                    expert_up(e + (NBLK - 1) * E, c)
                dve.wait_ge(acc_ready, NBLK)
                for t in range(BLK):
                    add_expert(e + (NBLK - 1) * E, e, t)
            finish(NBLK - 1)

        @block.gpsimd
        def _(pool):
            def root(which, tiles, step, eps_done, rstd_done, base):
                pool.wait_ge(step, 2 * base + 2)
                nc.gpsimd.tensor_tensor(var_eps[:, which, 0:tiles], moments[:, which, 0:tiles, 1], eps_row[:, 0:tiles],
                                        ALU.add).then_inc(eps_done, 1)
                pool.wait_ge(eps_done, base + 1)
                nc.gpsimd.tensor_tensor(rstd[:, which, 0:tiles], var_eps[:, which, 0:tiles], power[:, 0:tiles],
                                        ALU.pow).then_inc(rstd_done, 1)

            def attend(p, s):
                if s == X_STEP:
                    pool.wait_ge(x_loaded, 16 * (p + 1))
                    for j in range(PAIR):
                        i = nc.gpsimd.tensor_tensor(x_bo[:, j], x_in[:, j], bo_all[:], ALU.add)
                    i.then_inc(x_bo_ready, 1)
                if s == WO_STEP:
                    root(0, PAIR, ln1_step, ln1_eps, ln1_rstd, p)
                if s == REC_STEP:
                    pool.wait_ge(xa_step, 6 * p + 2)
                    pool.wait_ge(exps_ready, p + 1)
                    nc.gpsimd.tensor_tensor(mix_a, y1t[:], scan_a[:], ALU.add).then_inc(mix_a_ready, 1)
                if s == BACK_STEP:
                    root(1, PAIR, ln2_step, ln2_eps, ln2_rstd, p)

            def low(dst, src, hi, i):
                cols = slice(i * PW, (i + 1) * PW)
                return nc.gpsimd.tensor_tensor(dst[:, cols], src[:, cols], hi[:, cols].bitcast(F32), ALU.subtract)

            def split_w2(n, i):
                pool.wait_ge(w2_hi_ready, PIECES * n + (i + 1))
                low(w2_lo, w2_raw, w2_hi, i).then_inc(w2_ready, 1)

            def split_w1(n, i):
                pool.wait_ge(w1_hi_ready, PIECES * n + (i + 1))
                low(w1_lo, w1_raw, w1_hi, i).then_inc(w1_ready, 1)

            def finish(b):
                root(2, BLK, ln3_step, ln3_eps, ln3_rstd, b)

            nc.gpsimd.memset(ident[:], 0.0).then_inc(masks_made, 1)
            nc.gpsimd.memset(head_mask[:], 1.0).then_inc(masks_made, 1)
            nc.gpsimd.memset(power[:], -0.5)
            nc.gpsimd.memset(eps_row[:], EPS).then_inc(masks_made, 1)
            pool.wait_ge(masks_made, 3)
            nc.gpsimd.affine_select(out=ident[:], in_=ident[:], compare_op=ALU.not_equal, fill=1.0,
                                    base=0, pattern=[[-1, P]], channel_multiplier=1).then_inc(masks_made, 1)
            nc.gpsimd.affine_select(out=head_mask[:], in_=head_mask[:], compare_op=ALU.is_ge, fill=0.0,
                                    base=0, pattern=[[-DH, HC]], channel_multiplier=1).then_inc(masks_made, 1)
            pool.wait_ge(masks_made, 5)
            nc.gpsimd.affine_select(out=head_mask[:], in_=head_mask[:], compare_op=ALU.is_ge, fill=0.0,
                                    base=DH - 1, pattern=[[DH, HC]], channel_multiplier=-1).then_inc(masks_made, 1)
            pool.wait_ge(consts_loaded, 16 * CONSTS)
            for i in range(PIECES):
                split_w1(0, i)
            with pool.Fori(0, 2) as p:
                for s in range(STEPS):
                    attend(p, s)
            with pool.Fori(0, NBLK - 1) as b:
                with pool.Fori(0, E // SC) as half:
                    for k in range(SC):
                        for c in range(FC):
                            if c < PIECES:
                                split_w2(b * E + half * SC + k, c)
                            attend(2 * b + half + 2, k * SLOTS + c)
                        for t in range(BLK):
                            split_w1(b * E + half * SC + (k + 1), t)
                            attend(2 * b + half + 2, k * SLOTS + FC + t)
                finish(b)
            with pool.Fori(0, E - 1) as e:
                for i in range(PIECES):
                    split_w2(e + (NBLK - 1) * E, i)
                for i in range(PIECES):
                    split_w1(e + ((NBLK - 1) * E + 1), i)
            for i in range(PIECES):
                split_w2(NBLK * E - 1, i)
            finish(NBLK - 1)


X_STEP, QK_STEP, V_STEP = 0, 1, 2
SCORE_STEP = [6, 7, 16, 17]
EXP_STEP = [8, 9, 20, 21]
TURN_STEP = [10, 12, 22, 24]
VALUE_STEP = [11, 13, 23, 25]
ATT_STEP, WO_STEP, CTX_STEP, Y1_STEP = 27, 28, 29, 30
XEXP_STEP, REC_STEP, BACK_STEP = 32, 33, 37
MASKS = 6
DVE_SETUP = 4


def kernel(**inputs):
    import numpy as _np
    import concourse.bacc as _bacc
    from concourse.bass_utils import run_bass_kernel_spmd as _run

    a = {k.replace("L0_", ""): _np.asarray(v) for k, v in inputs.items()}
    D = a["x"].shape[2]
    E, F = a["ffn_b1"].shape
    by_in = lambda w: w.transpose(1, 0, 2).reshape(D, D)
    laid = {
        "x": a["x"], "ctx": a["ctx_1024"],
        "wq": by_in(a["attn_wq"]), "wk": by_in(a["attn_wk"]), "wv": by_in(a["attn_wv"]), "wo": a["attn_wo"].T,
        "cols": _np.stack([a[k].reshape(D // 128, 128).T for k in ("attn_bq", "attn_bk", "xattn_w", "xattn_u")], axis=1),
        "bv": a["attn_bv"].reshape(D), "bo": a["attn_bo"],
        "wg": a["ffn_Wg"].T.reshape(D // 128, 128, E),
        "w1": a["ffn_W1"],
        "b1": a["ffn_b1"].reshape(E, F // 128, 128).transpose(2, 0, 1).reshape(128, E * F // 128),
        "w2": a["ffn_W2"], "b2": a["ffn_b2"],
    }
    nc = _bacc.Bacc("TRN2", target_bir_lowering=False, num_devices=1)
    arrays, args = {}, []
    for name, v in laid.items():
        arrays[f"in_{name}_dram"] = _np.ascontiguousarray(v)
        args.append(nc.dram_tensor(f"in_{name}_dram", v.shape, mybir.dt.from_np(v.dtype), kind="ExternalInput").ap())
    out = nc.dram_tensor("out_dram", a["x"].shape, F32, kind="ExternalOutput").ap()
    decoder_layer(nc, *args, out)
    return _run(nc, [arrays], core_ids=[0]).results[0]["out_dram"]
```

```python
from contextlib import ExitStack

import concourse.bass as bass
from concourse import mybir

F32 = mybir.dt.float32
F32R = mybir.dt.float32r
F16 = mybir.dt.float16
BF16 = mybir.dt.bfloat16
ALU = mybir.AluOpType
ACT = mybir.ActivationFunctionType
AX_X = mybir.AxisListType.X

P = 128
EPS = 1e-5


def decoder_layer(nc, x, ctx_in, wq, wk, wv, wo, cols, bv, bo, wg, w1, b1, w2, b2, out):
    B, S, D = x.shape
    E, _, F = w1.shape
    H = 16
    DH = D // H
    C = D // P
    HC = H // C
    HQ = HC // 2
    FC = F // P
    PAIR = 2
    BLK = 4
    NPAIR = B // PAIR
    NBLK = B // BLK
    TOK = BLK * S
    VW = DH + 1
    QUADS = PAIR * C * 2
    UNITS = PAIR * C
    SC = 4
    SLOTS = FC + BLK
    STEPS = SC * SLOTS
    RING = 4
    PIECES = 4
    PW = C * F // PIECES
    assert S == P and C == 2 and DH == 16 and TOK == 512 and E == 2 * SC

    with ExitStack() as ctx:
        def sb(name, shape, dt=F32):
            return ctx.enter_context(nc.sbuf_tensor(name, shape, dt))

        def sem(name):
            return ctx.enter_context(nc.semaphore(name))

        ident = sb("ident", [P, P])
        head_mask = sb("head_mask", [P, HC])
        ramp = sb("ramp", [P, S])
        ones = sb("ones", [P, S])
        proj_hi = sb("proj_hi", [P, 4, C, D], F32R)
        proj_lo = sb("proj_lo", [P, 4, C, D], F32R)
        bqk = sb("bqk", [P, 2, C])
        bq_scaled = sb("bq_scaled", [P, C])
        bv_all = sb("bv_all", [P, D])
        bo_all = sb("bo_all", [P, D])
        wu = sb("wu", [P, 2, C])
        decay = sb("decay", [P, 2, C])
        decay_row = sb("decay_row", [P, 2, C, S])
        wg_raw = sb("wg_raw", [P, C, E])
        wg_hi = sb("wg_hi", [P, C, P], F32R)
        wg_lo = sb("wg_lo", [P, C, P], F32R)
        b1_all = sb("b1_all", [P, E * FC])
        b2_raw = sb("b2_raw", [E, D])
        b2_hi = sb("b2_hi", [E, D], F32R)
        b2_lo = sb("b2_lo", [E, D], F32R)
        power = sb("power", [P, BLK])
        eps_row = sb("eps_row", [P, BLK])

        x_in = sb("x_in", [P, PAIR, D])
        ctx_sb = sb("ctx_sb", [P, PAIR, D])
        x_bo = sb("x_bo", [P, PAIR, D])
        xt_hi = sb("xt_hi", [P, C, PAIR * S], F32R)
        xt_lo = sb("xt_lo", [P, C, PAIR * S], F32R)
        q_all = sb("q_all", [P, C, PAIR * S])
        q_hi = sb("q_hi", [P, C, PAIR * S], F32R)
        q_lo = sb("q_lo", [P, C, PAIR * S], F32R)
        k_both = sb("k_both", [P, 2, C, PAIR * S])
        k_hi = sb("k_hi", [P, C, PAIR * S], F32R)
        kd = sb("kd", [P, 2, PAIR, HC, S], F32R)
        v_all = sb("v_all", [P, PAIR, D])
        v_hi = sb("v_hi", [P, PAIR, H, VW], BF16)
        v_mid = sb("v_mid", [P, PAIR, H, VW], BF16)
        v_lo = sb("v_lo", [P, PAIR, H, VW], BF16)
        neg_max = sb("neg_max", [P, QUADS, HQ])
        probs = sb("probs", [P, 2, 2, HQ, S])
        pt_hi = sb("pt_hi", [P, 2, HQ, S], F16)
        pt_lo = sb("pt_lo", [P, 2, HQ, S], F16)
        inv_sum = sb("inv_sum", [P, UNITS, HC])
        att = sb("att", [P, PAIR, D])
        y1 = sb("y1", [P, PAIR, D])
        stats = sb("stats", [P, BLK, 6])
        moments = sb("moments", [P, 3, BLK, 2])
        spare = sb("spare", [P, 5])
        var_eps = sb("var_eps", [P, 3, BLK])
        rstd = sb("rstd", [P, 3, BLK])
        y1t = sb("y1t", [P, C, PAIR, S])
        ctx_t = sb("ctx_t", [P, C, PAIR, S])
        exp_k = sb("exp_k", [P, C, PAIR, S])
        exp_uk = sb("exp_uk", [P, C, PAIR, S])
        inc_a = sb("inc_a", [P, C, PAIR, S])
        inc_b = sb("inc_b", [P, C, PAIR, S])
        x2 = sb("x2", [P, BLK, D])

        x2t_hi = sb("x2t_hi", [P, C, TOK], F32R)
        x2t_lo = sb("x2t_lo", [P, C, TOK], F32R)
        logits = sb("logits", [P, BLK, E])
        route_exps = sb("route_exps", [P, BLK, E])
        route_max = sb("route_max", [P, BLK])
        route_sum = sb("route_sum", [P, BLK])
        route_inv = sb("route_inv", [P, BLK])
        next_gate = sb("next_gate", [P, BLK, E])
        gate = sb("gate", [P, BLK, E])
        w1_raw = sb("w1_raw", [P, C * F])
        w2_raw = sb("w2_raw", [P, C * F])
        w1_hi = sb("w1_hi", [P, C * F], F32R)
        w1_lo = sb("w1_lo", [P, C * F], F32R)
        w2_hi = sb("w2_hi", [P, C * F], F32R)
        w2_lo = sb("w2_lo", [P, C * F], F32R)
        h_all = sb("h_all", [P, RING, TOK])
        h_hi = sb("h_hi", [P, FC, TOK], F32R)
        h_lo = sb("h_lo", [P, FC, TOK], F32R)
        acc = sb("acc", [P, BLK, D])

        w1h = w1_hi[:].rearrange("p (c f) -> p c f", c=C)
        w1l = w1_lo[:].rearrange("p (c f) -> p c f", c=C)
        w2h = w2_hi[:].rearrange("p (c d) -> p c d", c=FC)
        w2l = w2_lo[:].rearrange("p (c d) -> p c d", c=FC)
        gt_hi = xt_hi[:].rearrange("p c n -> p (c n)")[0:E]
        gt_lo = xt_lo[:].rearrange("p c n -> p (c n)")[0:E]
        logits_t = exp_uk[:].rearrange("p c j t -> p (c j t)")
        scan_a, scan_b = inc_a, inc_b
        mix = exp_k[:]

        up_ps = [ctx.enter_context(nc.psum_tensor(f"up_ps{i}", [P, TOK], F32)) for i in range(2)]
        down_ps = [ctx.enter_context(nc.psum_tensor(f"down_ps{i}", [P, 512], F32)) for i in range(2)]
        bank = [ctx.enter_context(nc.psum_tensor(f"bank{i}", [P, 512], F32)) for i in range(4)]

        def by_chunk(t):
            return t[:].rearrange("p (c n) -> p c n", c=C)

        def by_head(t):
            return t[:].rearrange("p (h t) -> p h t", h=HQ)

        def by_tile(t):
            return t[:].rearrange("p (j d) -> p j d", j=PAIR)

        def by_cjt(t):
            return t[:].rearrange("p (c j t) -> p c j t", c=C, j=PAIR)

        consts_loaded = sem("consts_loaded")
        masks_made = sem("masks_made")
        proj_loaded = sem("proj_loaded")
        proj_hi_ready = sem("proj_hi_ready")
        proj_ready = sem("proj_ready")
        decay_ready = sem("decay_ready")
        dve_setup = sem("dve_setup")
        act_setup = sem("act_setup")
        x_loaded = sem("x_loaded")
        ctx_loaded = sem("ctx_loaded")
        xt_ps = sem("xt_ps")
        xt_hi_ready = sem("xt_hi_ready")
        xt_ready = sem("xt_ready")
        q_ps = sem("q_ps")
        k_ps = sem("k_ps")
        v_ps = sem("v_ps")
        q_hi_ready = sem("q_hi_ready")
        q_ready = sem("q_ready")
        k_hi_ready = sem("k_hi_ready")
        k_rest_ready = sem("k_rest_ready")
        kd_ready = sem("kd_ready")
        v_step = sem("v_step")
        scores_ps = sem("scores_ps")
        max_ready = sem("max_ready")
        shifted = sem("shifted")
        probs_ready = sem("probs_ready")
        pt_ps = sem("pt_ps")
        pt_hi_ready = sem("pt_hi_ready")
        pt_ready = sem("pt_ready")
        pv_ps = sem("pv_ps")
        inv_ready = sem("inv_ready")
        att_ready = sem("att_ready")
        att_t_ps = sem("att_t_ps")
        att_hi_ready = sem("att_hi_ready")
        att_t_ready = sem("att_t_ready")
        wo_ps = sem("wo_ps")
        x_bo_ready = sem("x_bo_ready")
        y1_sum = sem("y1_sum")
        ln1_step = sem("ln1_step")
        ln1_eps = sem("ln1_eps")
        ln1_rstd = sem("ln1_rstd")
        y1_ready = sem("y1_ready")
        ctx_t_ps = sem("ctx_t_ps")
        ctx_t_ready = sem("ctx_t_ready")
        y1t_ps = sem("y1t_ps")
        exps_ready = sem("exps_ready")
        xa_step = sem("xa_step")
        mix_a_ready = sem("mix_a_ready")
        mix_ready = sem("mix_ready")
        x2_ps = sem("x2_ps")
        ln2_step = sem("ln2_step")
        ln2_eps = sem("ln2_eps")
        ln2_rstd = sem("ln2_rstd")
        x2_ready = sem("x2_ready")
        x2t_ps = sem("x2t_ps")
        x2t_hi_ready = sem("x2t_hi_ready")
        x2t_ready = sem("x2t_ready")
        logits_t_ps = sem("logits_t_ps")
        logits_t_ready = sem("logits_t_ready")
        logits_ps = sem("logits_ps")
        route_step = sem("route_step")
        route_exp = sem("route_exp")
        gate_ready = sem("gate_ready")
        gates_taken = sem("gates_taken")
        gate_t_ps = sem("gate_t_ps")
        gate_hi_ready = sem("gate_hi_ready")
        gate_t_ready = sem("gate_t_ready")
        b2_ps = sem("b2_ps")
        stored = sem("stored")
        acc_free = sem("acc_free")
        x2_biased = sem("x2_biased")
        ln3_step = sem("ln3_step")
        ln3_eps = sem("ln3_eps")
        ln3_rstd = sem("ln3_rstd")
        out_ready = sem("out_ready")
        w1_loaded = sem("w1_loaded")
        w2_loaded = sem("w2_loaded")
        w1_hi_ready = sem("w1_hi_ready")
        w1_ready = sem("w1_ready")
        w2_hi_ready = sem("w2_hi_ready")
        w2_ready = sem("w2_ready")
        up_done = sem("up_done")
        gelu_done = sem("gelu_done")
        h_hi_ready = sem("h_hi_ready")
        h_ready = sem("h_ready")
        down_done = sem("down_done")
        added = sem("added")

        CONSTS = 8
        def first(p):
            return isinstance(p, int) and p == 0

        block = ctx.enter_context(nc.Block())


        @block.sync
        def _(sp):
            def load_pair(p):
                sp.wait_ge(xt_ps, p)
                sp.wait_ge(x_bo_ready, p)
                sp.dma_start(x_in[:], x[bass.ds(PAIR * p, PAIR)].rearrange("j s d -> s j d")).then_inc(x_loaded, 16)
                sp.wait_ge(ctx_t_ps, p)
                sp.dma_start(ctx_sb[:], ctx_in[bass.ds(PAIR * p, PAIR)].rearrange("j s d -> s j d")).then_inc(ctx_loaded, 16)

            def load_w1(e, n):
                sp.wait_ge(w1_ready, PIECES * n)
                w = w1[e] if isinstance(e, int) else w1[bass.ds(e, 1)].rearrange("a r f -> (a r) f")
                sp.dma_start(w1_raw[:].rearrange("p (c f) -> p c f", c=C), w.rearrange("(c p) f -> p c f", p=P))\
                    .then_inc(w1_loaded, 16)

            def load_w2(e, n):
                sp.wait_ge(w2_ready, PIECES * n)
                w = w2[e] if isinstance(e, int) else w2[bass.ds(e, 1)].rearrange("a r d -> (a r) d")
                sp.dma_start(w2_raw[:].rearrange("p (c d) -> p c d", c=FC), w.rearrange("(c p) d -> p c d", p=P))\
                    .then_inc(w2_loaded, 16)

            sp.dma_start(x_in[:], x[0:PAIR].rearrange("j s d -> s j d")).then_inc(x_loaded, 16)
            for i, w in enumerate((wq, wk, wv, wo)):
                sp.dma_start(w2_raw[:].rearrange("p (i c d) -> p i c d", i=4, c=C)[:, i],
                             w.rearrange("(c p) d -> p c d", p=P)).then_inc(proj_loaded, 16)
            sp.dma_start(bqk[:], cols[:, 0:2, :]).then_inc(consts_loaded, 16)
            sp.dma_start(wu[:], cols[:, 2:4, :]).then_inc(consts_loaded, 16)
            sp.dma_start(bv_all[:], bv.rearrange("(a d) -> a d", a=1).to_broadcast([P, D])).then_inc(consts_loaded, 16)
            sp.dma_start(bo_all[:], bo.rearrange("(a d) -> a d", a=1).to_broadcast([P, D])).then_inc(consts_loaded, 16)
            for c in range(C):
                sp.dma_start(wg_raw[:, c, :], wg[c]).then_inc(consts_loaded, 16)
            sp.dma_start(b1_all[:], b1).then_inc(consts_loaded, 16)
            sp.dma_start(b2_raw[:], b2).then_inc(consts_loaded, 16)
            sp.dma_start(ctx_sb[:], ctx_in[0:PAIR].rearrange("j s d -> s j d")).then_inc(ctx_loaded, 16)
            load_w1(0, 0)
            sp.wait_ge(proj_ready, PIECES)
            load_w2(0, 0)
            load_pair(1)

            with sp.Fori(0, NBLK - 1) as b:
                for e in range(E):
                    if e % SC == 0:
                        load_pair(2 * b + (e // SC + 2))
                    load_w1((e + 1) % E, b * E + (e + 1))
                    load_w2((e + 1) % E, b * E + (e + 1))
            with sp.Fori(0, E - 1) as e:
                load_w1(e + 1, e + ((NBLK - 1) * E + 1))
                load_w2(e + 1, e + ((NBLK - 1) * E + 1))

        @block.tensor
        def _(pe):
            def product(ps, hi, lo, rhs_hi, rhs_lo, first=True, last=True):
                nc.tensor.matmul(ps, hi, rhs_hi, start=first, stop=False)
                nc.tensor.matmul(ps, hi, rhs_lo, start=False, stop=False)
                return nc.tensor.matmul(ps, lo, rhs_hi, start=False, stop=last)

            def project(ps, which, c):
                for kc in range(C):
                    cols = slice(c * P, (c + 1) * P)
                    mm = product(ps, proj_hi[:, which, kc, cols], proj_lo[:, which, kc, cols],
                                 xt_hi[:, kc, :], xt_lo[:, kc, :], kc == 0, kc == C - 1)
                return mm

            def project_rows(ps, which, j):
                for kc in range(C):
                    rows = slice(j * S, (j + 1) * S)
                    mm = product(ps, xt_hi[:, kc, rows], xt_lo[:, kc, rows],
                                 proj_hi[:, which, kc, :], proj_lo[:, which, kc, :], kc == 0, kc == C - 1)
                return mm

            def turn(dst, src):
                for c in range(C):
                    for j in range(PAIR):
                        mm = nc.tensor.transpose(dst[:, c, j * S:(j + 1) * S], src[:, j, c * P:(c + 1) * P], ident[:])
                return mm

            def scores(p, u):
                c, j = divmod(u, PAIR)
                if j == 0:
                    pe.wait_ge(kd_ready, C * p + (c + 1))
                rows = slice(j * S, (j + 1) * S)
                if u == 2:
                    pe.wait_ge(att_ready, UNITS * p + 2)
                for i in range(2):
                    if u % 2:
                        pe.wait_ge(shifted, QUADS * p + (2 * u - 1 + i))
                    heads = slice(i * HQ, (i + 1) * HQ)
                    product(by_head(bank[i]), q_hi[:, c, rows], q_lo[:, c, rows],
                            kd[:, 0, j, heads, :], kd[:, 1, j, heads, :]).then_inc(scores_ps, 1)

            def turn_probs(p, u):
                if u == 0 and not first(p):
                    pe.wait_ge(x2_ready, p)
                for i in range(2):
                    g = 2 * u + i
                    pe.wait_ge(probs_ready, QUADS * p + (g + 1))
                    for h in range(HQ):
                        mm = nc.tensor.transpose(by_head(bank[2 + i])[:, h, :], probs[:, u % 2, i, h, :], ident[:])
                    mm.then_inc(pt_ps, 1)

            def weigh_values(p, u):
                c, j = divmod(u, PAIR)
                if u == 0:
                    pe.wait_ge(v_step, 5 * (p + 1))
                if u % 2 == 0:
                    pe.wait_ge(shifted, QUADS * p + (2 * u + 4))
                for i in range(2):
                    pe.wait_ge(pt_ready, QUADS * p + (2 * u + i + 1))
                    for h in range(HQ):
                        slot = i * HQ + h
                        ps = bank[u % 2][:, slot * VW:(slot + 1) * VW]
                        head = c * HC + i * HQ + h
                        hi, lo = pt_hi[:, i, h, :], pt_lo[:, i, h, :]
                        nc.tensor.matmul(ps, hi, v_hi[:, j, head, :], start=True, stop=False)
                        nc.tensor.matmul(ps, hi, v_mid[:, j, head, :], start=False, stop=False)
                        nc.tensor.matmul(ps, hi, v_lo[:, j, head, :], start=False, stop=False)
                        nc.tensor.matmul(ps, lo, v_hi[:, j, head, :], start=False, stop=False)
                        mm = nc.tensor.matmul(ps, lo, v_mid[:, j, head, :], start=False, stop=True)
                    mm.then_inc(pv_ps, 1)

            def attend(p, s):
                if s == X_STEP:
                    pe.wait_ge(x_loaded, 16 * (p + 1))
                    turn(by_chunk(bank[0]), x_in).then_inc(xt_ps, 1)
                if s == QK_STEP:
                    if first(p):
                        pe.wait_ge(proj_ready, PIECES)
                    else:
                        pe.wait_ge(ctx_t_ready, p)
                    pe.wait_ge(xt_ready, p + 1)
                    project(by_chunk(bank[1])[:, 0, :], 0, 0)
                    project(by_chunk(bank[1])[:, 1, :], 0, 1).then_inc(q_ps, 1)
                    project(by_chunk(bank[2])[:, 0, :], 1, 0)
                    project(by_chunk(bank[2])[:, 1, :], 1, 1).then_inc(k_ps, 1)
                if s == V_STEP:
                    if not first(p):
                        pe.wait_ge(y1_sum, p)
                    project_rows(by_tile(bank[3])[:, 0, :], 2, 0)
                    project_rows(by_tile(bank[3])[:, 1, :], 2, 1).then_inc(v_ps, 1)
                if s == SCORE_STEP[0]:
                    pe.wait_ge(q_ready, p + 1)
                    if not first(p):
                        pe.wait_ge(exps_ready, p)
                for u in range(UNITS):
                    if s == SCORE_STEP[u]:
                        scores(p, u)
                    if s == TURN_STEP[u]:
                        turn_probs(p, u)
                    if s == VALUE_STEP[u]:
                        weigh_values(p, u)
                if s == ATT_STEP:
                    pe.wait_ge(att_ready, UNITS * (p + 1))
                    turn(by_chunk(bank[2]), att).then_inc(att_t_ps, 1)
                if s == WO_STEP:
                    pe.wait_ge(att_t_ready, p + 1)
                    project_rows(by_tile(bank[3])[:, 0, :], 3, 0)
                    project_rows(by_tile(bank[3])[:, 1, :], 3, 1).then_inc(wo_ps, 1)
                if s == CTX_STEP:
                    pe.wait_ge(ctx_loaded, 16 * (p + 1))
                    turn(by_chunk(bank[1]), ctx_sb).then_inc(ctx_t_ps, 1)
                if s == Y1_STEP:
                    pe.wait_ge(y1_ready, p + 1)
                    turn(by_chunk(bank[0]), y1).then_inc(y1t_ps, 1)
                if s == BACK_STEP:
                    pe.wait_ge(mix_ready, p + 1)
                    for j in range(PAIR):
                        for c in range(C):
                            mm = nc.tensor.transpose(by_tile(bank[2])[:, j, c * P:(c + 1) * P], mix[:, c, j, :], ident[:])
                    mm.then_inc(x2_ps, 1)

            def route(b, part):
                if part == 0:
                    pe.wait_ge(x2_ready, 2 * (b + 1))
                    for c in range(C):
                        for t in range(BLK):
                            mm = nc.tensor.transpose(bank[c][:, t * S:(t + 1) * S], x2[:, t, c * P:(c + 1) * P], ident[:])
                        mm.then_inc(x2t_ps, 1)
                if part == 1:
                    if first(b):
                        pe.wait_ge(dve_setup, DVE_SETUP)
                    pe.wait_ge(x2t_ready, C * (b + 1))
                    for kc in range(C):
                        mm = product(bank[2][:], wg_hi[:, kc, :], wg_lo[:, kc, :],
                                     x2t_hi[:, kc, :], x2t_lo[:, kc, :], kc == 0, kc == C - 1)
                    mm.then_inc(logits_t_ps, 1)
                if part == 2:
                    pe.wait_ge(logits_t_ready, b + 1)
                    for t in range(BLK):
                        mm = nc.tensor.transpose(bank[3][:, t * P:(t + 1) * P], logits_t[:, t * S:(t + 1) * S], ident[:])
                    mm.then_inc(logits_ps, 1)
                if part == 3:
                    pe.wait_ge(gate_ready, b + 1)
                    for t in range(BLK):
                        mm = nc.tensor.transpose(bank[2][0:E, t * S:(t + 1) * S], next_gate[:, t, :], ident[:])
                    mm.then_inc(gate_t_ps, 1)
                if part == 4:
                    pe.wait_ge(gate_t_ready, b + 1)
                    for t in range(BLK):
                        rows = slice(t * S, (t + 1) * S)
                        mm = product(by_tile(bank[t // 2])[:, t % 2, :], gt_hi[:, rows], gt_lo[:, rows], b2_hi[:], b2_lo[:])
                    mm.then_inc(b2_ps, 1)

            def up(n, c):
                if c == 0:
                    pe.wait_ge(w1_ready, PIECES * (n + 1))
                if c >= 2:
                    pe.wait_ge(gelu_done, FC * n + (c - 1))
                cols = slice(c * P, (c + 1) * P)
                for kc in range(C):
                    mm = product(up_ps[c % 2][:], w1h[:, kc, cols], w1l[:, kc, cols],
                                 x2t_hi[:, kc, :], x2t_lo[:, kc, :], kc == 0, kc == C - 1)
                mm.then_inc(up_done, 1)

            def down(n, t):
                if t == 0:
                    pe.wait_ge(w2_ready, PIECES * (n + 1))
                if t >= 2:
                    pe.wait_ge(added, BLK * n + (t - 1))
                rows = slice(t * S, (t + 1) * S)
                for c in range(FC):
                    if t == 0:
                        pe.wait_ge(h_ready, FC * n + (c + 1))
                    mm = product(down_ps[t % 2][:, 0:D], h_hi[:, c, rows], h_lo[:, c, rows],
                                 w2h[:, c, :], w2l[:, c, :], c == 0, c == FC - 1)
                mm.then_inc(down_done, 1)

            pe.wait_ge(masks_made, MASKS)
            for p, s in ALONE:
                attend(p, s)
            for part in range(ROUTE_PARTS):
                route(0, part)
            with pe.Fori(0, NBLK - 1) as b:
                for e in range(E):
                    half, k = divmod(e, SC)
                    for c in range(FC):
                        up(b * E + e, c)
                        if (e, c) == (0, 0):
                            pe.wait_ge(x2_biased, b + 1)
                        attend(2 * b + (half + 2), k * SLOTS + c)
                    if e == E - 1:
                        route(b + 1, 0)
                    for t in range(BLK):
                        down(b * E + e, t)
                        attend(2 * b + (half + 2), k * SLOTS + FC + t)
                        if e == E - 1:
                            route(b + 1, t + 1)
            with pe.Fori(0, E) as e:
                for c in range(FC):
                    up(e + (NBLK - 1) * E, c)
                for t in range(BLK):
                    down(e + (NBLK - 1) * E, t)

        @block.scalar
        def _(act):
            def split_hi(dst, src, i):
                cols = slice(i * PW, (i + 1) * PW)
                return nc.scalar.activation(dst[:, cols], src[:, cols], ACT.Copy)

            def attend(p, s):
                if s == X_STEP:
                    act.wait_ge(xt_ps, p + 1)
                    nc.scalar.activation(xt_hi[:], by_chunk(bank[0]), ACT.Copy).then_inc(xt_hi_ready, 1)
                if s == QK_STEP:
                    act.wait_ge(q_ps, p + 1)
                    for dst in (q_all, q_hi):
                        for c in range(C):
                            a = nc.scalar.activation(dst[:, c, :], by_chunk(bank[1])[:, c, :], ACT.Identity,
                                                     bias=bq_scaled[:, c:c + 1], scale=DH ** -0.5)
                    a.then_inc(q_hi_ready, 1)
                    act.wait_ge(k_ps, p + 1)
                    for dst in (k_both[:, 0], k_hi):
                        for c in range(C):
                            a = nc.scalar.activation(dst[:, c, :], by_chunk(bank[2])[:, c, :], ACT.Identity,
                                                     bias=bqk[:, 1, c:c + 1])
                    a.then_inc(k_hi_ready, 1)
                for u in range(UNITS):
                    if s == EXP_STEP[u]:
                        for i in range(2):
                            act.wait_ge(shifted, QUADS * p + (2 * u + i + 1))
                            nc.scalar.activation(probs[:, u % 2, i], probs[:, u % 2, i], ACT.Exp).then_inc(probs_ready, 1)
                    if s == TURN_STEP[u]:
                        for i in range(2):
                            g = 2 * u + i
                            act.wait_ge(pt_ps, QUADS * p + (g + 1))
                            if u > 0:
                                act.wait_ge(pv_ps, QUADS * p + (g - 1))
                            nc.scalar.activation(pt_hi[:, i], by_head(bank[2 + i]), ACT.Copy).then_inc(pt_hi_ready, 1)
                if s == ATT_STEP:
                    act.wait_ge(att_t_ps, p + 1)
                    nc.scalar.activation(xt_hi[:], by_chunk(bank[2]), ACT.Copy).then_inc(att_hi_ready, 1)
                if s == CTX_STEP:
                    act.wait_ge(ctx_t_ps, p + 1)
                    nc.scalar.activation(ctx_t[:], by_cjt(bank[1]), ACT.Copy).then_inc(ctx_t_ready, 1)
                if s == XEXP_STEP:
                    act.wait_ge(y1t_ps, p + 1)
                    k = by_cjt(bank[0])
                    nc.scalar.activation(y1t[:], k, ACT.Copy)
                    nc.scalar.activation(exp_k[:], k, ACT.Exp)
                    nc.scalar.activation(inc_b[:, :, :, 2:S], k[:, :, :, 1:S - 1], ACT.Exp, scale=-1.0)
                    for c in range(C):
                        a = nc.scalar.activation(exp_uk[:, c], k[:, c], ACT.Exp, bias=wu[:, 1, c:c + 1])
                    a.then_inc(exps_ready, 1)

            def route(b, part):
                if part == 0:
                    for c in range(C):
                        act.wait_ge(x2t_ps, C * b + (c + 1))
                        nc.scalar.activation(x2t_hi[:, c, :], bank[c][:], ACT.Copy).then_inc(x2t_hi_ready, 1)
                if part == 1:
                    act.wait_ge(logits_t_ps, b + 1)
                    nc.scalar.activation(logits_t, bank[2][:], ACT.Copy).then_inc(logits_t_ready, 1)
                if part == 2:
                    act.wait_ge(route_step, 4 * b + 2)
                    nc.scalar.activation(route_exps[:], logits[:], ACT.Exp).then_inc(route_exp, 1)
                if part == 3:
                    act.wait_ge(gate_t_ps, b + 1)
                    nc.scalar.activation(gt_hi, bank[2][0:E, :], ACT.Copy).then_inc(gate_hi_ready, 1)

            def hidden_hi(n, c):
                act.wait_ge(gelu_done, FC * n + (c + 1))
                nc.scalar.activation(h_hi[:, c, :], h_all[:, c % RING, :], ACT.Copy).then_inc(h_hi_ready, 1)

            def hidden(n, e, c):
                act.wait_ge(up_done, FC * n + (c + 1))
                if c >= RING:
                    act.wait_ge(h_ready, FC * n + (c - RING + 1))
                nc.scalar.activation(h_all[:, c % RING, :], up_ps[c % 2][:], ACT.Gelu_apprx_tanh,
                                     bias=b1_all[:, e * FC + c:e * FC + c + 1] if isinstance(e, int) else b1_all[:, bass.ds(e * FC + c, 1)]).then_inc(gelu_done, 1)
                if c > 0:
                    hidden_hi(n, c - 1)
                if c == FC - 1:
                    hidden_hi(n, c)

            def split_w1(n, i):
                if i == 0:
                    act.wait_ge(w1_loaded, 16 * (n + 1))
                    if not isinstance(n, int):
                        act.wait_ge(up_done, FC * n)
                split_hi(w1_hi, w1_raw, i).then_inc(w1_hi_ready, 1)

            act.wait_ge(consts_loaded, 16 * CONSTS)
            nc.scalar.activation(decay[:, 0, :], wu[:, 0, :], ACT.Exp, scale=-1.0)
            nc.scalar.activation(decay[:, 1, :], wu[:, 0, :], ACT.Exp).then_inc(decay_ready, 1)
            nc.scalar.activation(bq_scaled[:], bqk[:, 0, :], ACT.Copy, scale=DH ** -0.5).then_inc(act_setup, 1)
            nc.scalar.activation(b2_hi[:], b2_raw[:], ACT.Copy).then_inc(act_setup, 1)
            act.wait_ge(dve_setup, 1)
            nc.scalar.activation(wg_hi[:, :, 0:E], wg_raw[:], ACT.Copy).then_inc(act_setup, 1)
            act.wait_ge(proj_loaded, 16 * 4)
            for i in range(4):
                nc.scalar.activation(proj_hi[:, i], w2_raw[:].rearrange("p (i c d) -> p i c d", i=4, c=C)[:, i],
                                     ACT.Copy).then_inc(proj_hi_ready, 1)
            for i in range(PIECES):
                split_w1(0, i)
            act.wait_ge(act_setup, 3)
            for p, s in ALONE:
                attend(p, s)
            for part in range(ROUTE_PARTS):
                route(0, part)
            with act.Fori(0, NBLK - 1) as b:
                for e in range(E):
                    half, k = divmod(e, SC)
                    for c in range(FC):
                        hidden(b * E + e, e, c)
                        attend(2 * b + (half + 2), k * SLOTS + c)
                    if e == E - 1:
                        route(b + 1, 0)
                    for t in range(BLK):
                        if t < PIECES // 2:
                            split_w1(b * E + (e + 1), 2 * t)
                            split_w1(b * E + (e + 1), 2 * t + 1)
                        attend(2 * b + (half + 2), k * SLOTS + FC + t)
                        if e == E - 1:
                            route(b + 1, t + 1)
            nc.scalar.activation(spare[:, 4:5], spare[:, 3:4], ACT.Gelu_apprx_tanh)
            with act.Fori(0, E - 1) as e:
                for c in range(FC):
                    hidden(e + (NBLK - 1) * E, e, c)
                for i in range(PIECES):
                    split_w1(e + ((NBLK - 1) * E + 1), i)
            for c in range(FC):
                hidden(NBLK * E - 1, E - 1, c)

        @block.vector
        def _(dve):
            def low(dst, src, hi):
                return nc.vector.tensor_tensor(dst, src, hi.bitcast(F32), ALU.subtract)

            def moments_of(src, which, step, base):
                tiles = len(src)
                for j in range(tiles):
                    i = nc.vector.bn_stats(stats[:, j, :], src[j])
                i.then_inc(step, 1)
                dve.wait_ge(step, 2 * base + 1)
                nc.vector.tensor_copy(spare[:, which:which + 1], stats[:, 0, 1:2])
                for j in range(tiles):
                    i = nc.vector.bn_aggr(moments[:, which, j, :], stats[:, j, :])
                i.then_inc(step, 1)

            def norm(src, dst, which, rstd_done, base):
                dve.wait_ge(rstd_done, base + 1)
                for j in range(len(src)):
                    i = nc.vector.tensor_scalar(dst[j], src[j], moments[:, which, j, 0:1], rstd[:, which, j:j + 1],
                                                ALU.subtract, ALU.mult)
                return i

            def diagonal(p, c):
                if c > 0:
                    dve.wait_ge(scores_ps, QUADS * p + 2 * PAIR * c)
                for h in range(HC):
                    i = nc.vector.tensor_scalar(kd[:, :, :, h, :], k_both[:, :, c, :].rearrange("p a (j t) -> p a j t", j=PAIR),
                                                head_mask[:, h:h + 1], None, ALU.mult)
                i.then_inc(kd_ready, 1)

            def heads(t):
                return t[:].rearrange("p j (h e) -> p j h e", h=H)

            def attend(p, half, s):
                if s == X_STEP:
                    dve.wait_ge(xt_hi_ready, p + 1)
                    low(xt_lo[:], by_chunk(bank[0]), xt_hi[:]).then_inc(xt_ready, 1)
                if s == QK_STEP:
                    dve.wait_ge(q_hi_ready, p + 1)
                    low(q_lo[:], q_all[:], q_hi[:]).then_inc(q_ready, 1)
                    dve.wait_ge(k_hi_ready, p + 1)
                    low(k_both[:, 1], k_both[:, 0], k_hi[:]).then_inc(k_rest_ready, 1)
                    dve.wait_ge(k_rest_ready, p + 1)
                    diagonal(p, 0)
                if s == V_STEP:
                    dve.wait_ge(v_ps, p + 1)
                    for j in range(PAIR):
                        i = nc.vector.tensor_tensor(v_all[:, j], by_tile(bank[3])[:, j], bv_all[:], ALU.add)
                    i.then_inc(v_step, 1)
                if s == VSPLIT_STEP:
                    dve.wait_ge(v_step, 5 * p + 1)
                    nc.vector.tensor_copy(v_hi[:, :, :, 0:DH], heads(v_all)).then_inc(v_step, 1)
                    dve.wait_ge(v_step, 5 * p + 2)
                    nc.vector.tensor_tensor(heads(v_all), heads(v_all), v_hi[:, :, :, 0:DH], ALU.subtract).then_inc(v_step, 1)
                    dve.wait_ge(v_step, 5 * p + 3)
                    nc.vector.tensor_copy(v_mid[:, :, :, 0:DH], heads(v_all)).then_inc(v_step, 1)
                    dve.wait_ge(v_step, 5 * p + 4)
                    nc.vector.tensor_tensor(v_lo[:, :, :, 0:DH], heads(v_all), v_mid[:, :, :, 0:DH], ALU.subtract).then_inc(v_step, 1)
                for u in range(UNITS):
                    c, j = divmod(u, PAIR)
                    if s == SCORE_STEP[u]:
                        for i in range(2):
                            g = 2 * u + i
                            dve.wait_ge(scores_ps, QUADS * p + (g + 1))
                            nc.vector.tensor_reduce(neg_max[:, g, :], by_head(bank[i]), AX_X, ALU.max,
                                                    negate=True).then_inc(max_ready, 1)
                        for i in range(2):
                            g = 2 * u + i
                            dve.wait_ge(max_ready, QUADS * p + (g + 1))
                            if u >= 2:
                                dve.wait_ge(pt_ps, QUADS * p + (g - 3))
                            nc.vector.tensor_tensor(probs[:, u % 2, i], by_head(bank[i]),
                                                    neg_max[:, g, :].rearrange("p (h a) -> p h a", a=1).to_broadcast([P, HQ, S]),
                                                    ALU.add).then_inc(shifted, 1)
                    if s == SCORE_STEP[u] + 1 and u == PAIR - 1:
                        diagonal(p, 1)
                    if s == TURN_STEP[u]:
                        for i in range(2):
                            g = 2 * u + i
                            dve.wait_ge(pt_hi_ready, QUADS * p + (g + 1))
                            nc.vector.tensor_tensor(pt_lo[:, i], by_head(bank[2 + i]), pt_hi[:, i], ALU.subtract)\
                                .then_inc(pt_ready, 1)
                    if s == VALUE_STEP[u]:
                        dve.wait_ge(pv_ps, QUADS * p + (2 * u + 2))
                        rows = bank[u % 2][:, 0:HC * VW].rearrange("p (h e) -> p h e", h=HC)
                        nc.vector.reciprocal(inv_sum[:, u, :], rows[:, :, DH]).then_inc(inv_ready, 1)
                        dve.wait_ge(inv_ready, UNITS * p + (u + 1))
                        nc.vector.tensor_tensor(att[:, j, c * P:(c + 1) * P].rearrange("p (h e) -> p h e", h=HC), rows[:, :, 0:DH],
                                                inv_sum[:, u, :].rearrange("p (h a) -> p h a", a=1).to_broadcast([P, HC, DH]),
                                                ALU.mult).then_inc(att_ready, 1)
                if s == ATT_STEP:
                    dve.wait_ge(att_hi_ready, p + 1)
                    low(xt_lo[:], by_chunk(bank[2]), xt_hi[:]).then_inc(att_t_ready, 1)
                if s == WO_STEP:
                    dve.wait_ge(wo_ps, p + 1)
                    dve.wait_ge(x_bo_ready, p + 1)
                    nc.vector.tensor_tensor(y1[:], by_tile(bank[3]), x_bo[:], ALU.add).then_inc(y1_sum, 1)
                    dve.wait_ge(y1_sum, p + 1)
                    moments_of([y1[:, j] for j in range(PAIR)], 0, ln1_step, p)
                if s == NORM1_STEP:
                    tiles = [y1[:, j] for j in range(PAIR)]
                    norm(tiles, tiles, 0, ln1_rstd, p).then_inc(y1_ready, 1)
                if s == REC_STEP:
                    dve.wait_ge(exps_ready, p + 1)
                    dve.wait_ge(ctx_t_ready, p + 1)
                    nc.vector.tensor_tensor(inc_a[:, :, :, 2:S], exp_k[:, :, :, 1:S - 1], ctx_t[:, :, :, 1:S - 1],
                                            ALU.mult).then_inc(xa_step, 1)
                    dve.wait_ge(xa_step, 6 * p + 1)
                    for i, (state, inc) in enumerate(((scan_a, inc_a), (scan_b, inc_b))):
                        for c in range(C):
                            for j in range(PAIR):
                                o = nc.vector.tensor_tensor_scan(state[:, c, j, :], decay_row[:, i, c, :], inc[:, c, j, :],
                                                                 0.0, ALU.mult, ALU.add)
                        o.then_inc(xa_step, 1)
                    flat = mix.rearrange("p c j t -> p (c j) t")
                    dve.wait_ge(xa_step, 6 * p + 3)
                    nc.vector.tensor_tensor(mix, ctx_t[:], scan_b[:], ALU.mult).then_inc(xa_step, 1)
                    dve.wait_ge(xa_step, 6 * p + 4)
                    nc.vector.tensor_tensor(flat, flat, ramp[:].rearrange("p (a t) -> p a t", a=1).to_broadcast([P, C * PAIR, S]),
                                            ALU.add).then_inc(xa_step, 1)
                    dve.wait_ge(xa_step, 6 * p + 5)
                    nc.vector.tensor_tensor(mix, mix, exp_uk[:], ALU.mult).then_inc(xa_step, 1)
                    dve.wait_ge(xa_step, 6 * p + 6)
                    dve.wait_ge(mix_a_ready, p + 1)
                    nc.vector.tensor_tensor(mix, mix, y1t[:], ALU.add).then_inc(mix_ready, 1)
                if s == BACK_STEP:
                    dve.wait_ge(x2_ps, p + 1)
                    moments_of([by_tile(bank[2])[:, j] for j in range(PAIR)], 1, ln2_step, p)
                if s == NORM2_STEP:
                    norm([by_tile(bank[2])[:, j] for j in range(PAIR)], [x2[:, PAIR * half + j] for j in range(PAIR)],
                         1, ln2_rstd, p).then_inc(x2_ready, 1)

            def over_experts(v):
                return v[:].rearrange("p (t a) -> p t a", a=1).to_broadcast([P, BLK, E])

            def route(b, part):
                if part == 0:
                    for c in range(C):
                        dve.wait_ge(x2t_hi_ready, C * b + (c + 1))
                        low(x2t_lo[:, c, :], bank[c][:], x2t_hi[:, c, :]).then_inc(x2t_ready, 1)
                if part == 2:
                    dve.wait_ge(logits_ps, b + 1)
                    lg = bank[3][:].rearrange("p (t e) -> p t e", t=BLK)[:, :, 0:E]
                    nc.vector.tensor_reduce(route_max[:], lg, AX_X, ALU.max, negate=True).then_inc(route_step, 1)
                    dve.wait_ge(route_step, 4 * b + 1)
                    nc.vector.tensor_tensor(logits[:], lg, over_experts(route_max), ALU.add).then_inc(route_step, 1)
                    dve.wait_ge(route_exp, b + 1)
                    nc.vector.tensor_reduce(route_sum[:], route_exps[:], AX_X, ALU.add).then_inc(route_step, 1)
                    dve.wait_ge(route_step, 4 * b + 3)
                    nc.vector.reciprocal(route_inv[:], route_sum[:]).then_inc(route_step, 1)
                if part == 3:
                    dve.wait_ge(route_step, 4 * b + 4)
                    nc.vector.tensor_tensor(next_gate[:], route_exps[:], over_experts(route_inv), ALU.mult).then_inc(gate_ready, 1)
                    dve.wait_ge(gate_hi_ready, b + 1)
                    low(gt_lo, bank[2][0:E, :], gt_hi).then_inc(gate_t_ready, 1)
                if part == 4:
                    dve.wait_ge(b2_ps, b + 1)
                    for i in range(2):
                        pair = x2[:, 2 * i:2 * i + 2, :]
                        o = nc.vector.tensor_tensor(pair, by_tile(bank[i]), pair, ALU.add)
                    o.then_inc(x2_biased, 1)

            def take_gates(b):
                dve.wait_ge(gate_ready, b + 1)
                nc.vector.tensor_copy(gate[:], next_gate[:]).then_inc(gates_taken, 1)

            def hidden_lo(n, c):
                dve.wait_ge(h_hi_ready, FC * n + (c + 1))
                low(h_lo[:, c, :], h_all[:, c % RING, :], h_hi[:, c, :]).then_inc(h_ready, 1)

            def add_expert(n, e, t, first=False):
                dve.wait_ge(down_done, BLK * n + (t + 1))
                weight = gate[:, t, e:e + 1] if isinstance(e, int) else gate[:, t, bass.ds(e, 1)]
                nc.vector.scalar_tensor_tensor(out=acc[:, t, :], in0=down_ps[t % 2][:, 0:D], scalar=weight,
                                               in1=x2[:, t, :] if first else acc[:, t, :],
                                               op0=ALU.mult, op1=ALU.add).then_inc(added, 1)

            def expert_up(n, c):
                if c < PIECES:
                    if c == 0:
                        dve.wait_ge(w2_loaded, 16 * (n + 1))
                    cols = slice(c * PW, (c + 1) * PW)
                    nc.vector.tensor_copy(w2_hi[:, cols], w2_raw[:, cols]).then_inc(w2_hi_ready, 1)
                if c > 0:
                    hidden_lo(n, c - 1)
                if c == FC - 1:
                    hidden_lo(n, c)

            def finish(b):
                dve.wait_ge(added, BLK * E * (b + 1))
                tiles = [acc[:, t] for t in range(BLK)]
                moments_of(tiles, 2, ln3_step, b)
                norm(tiles, tiles, 2, ln3_rstd, b).then_inc(out_ready, 1)

            nc.vector.memset(wg_hi[:].bitcast(F32), 0.0)
            nc.vector.memset(spare[:], 0.0)
            nc.vector.memset(wg_lo[:].bitcast(F32), 0.0).then_inc(dve_setup, 1)
            nc.vector.memset(inc_a[:, :, :, 0:2], 0.0)
            nc.vector.memset(inc_b[:, :, :, 0:2], 0.0)
            nc.vector.memset(v_hi[:, :, :, DH:VW], 1.0)
            nc.vector.memset(v_mid[:, :, :, DH:VW], 0.0)
            nc.vector.memset(v_lo[:, :, :, DH:VW], 0.0)
            nc.vector.memset(ones[:], 1.0).then_inc(dve_setup, 1)
            dve.wait_ge(dve_setup, 2)
            nc.vector.tensor_tensor_scan(ramp[:], ones[:], ones[:], 0.0, ALU.mult, ALU.add).then_inc(dve_setup, 1)
            dve.wait_ge(dve_setup, 3)
            nc.vector.tensor_scalar(ramp[:], ramp[:], -2.0, 0.0, ALU.add, ALU.max)
            dve.wait_ge(decay_ready, 1)
            for i in range(2):
                for c in range(C):
                    nc.vector.tensor_scalar(decay_row[:, i, c, :], ones[:], decay[:, i, c:c + 1], None, ALU.mult)
            dve.wait_ge(act_setup, 3)
            low(wg_lo[:, :, 0:E], wg_raw[:], wg_hi[:, :, 0:E])
            low(b2_lo[:], b2_raw[:], b2_hi[:]).then_inc(dve_setup, 1)
            for i in range(PIECES):
                dve.wait_ge(proj_hi_ready, i + 1)
                low(proj_lo[:, i], w2_raw[:].rearrange("p (i c d) -> p i c d", i=4, c=C)[:, i], proj_hi[:, i])\
                    .then_inc(proj_ready, 1)
            dve.wait_ge(masks_made, MASKS)
            dve.wait_ge(dve_setup, DVE_SETUP)
            for p, s in ALONE:
                attend(p, p, s)
            for part in range(ROUTE_PARTS):
                route(0, part)
            take_gates(0)
            with dve.Fori(0, NBLK - 1) as b:
                dve.wait_ge(x2_biased, b + 1)
                dve.wait_ge(gates_taken, b + 1)
                for e in range(E):
                    half, k = divmod(e, SC)
                    for c in range(FC):
                        expert_up(b * E + e, c)
                        attend(2 * b + (half + 2), half, k * SLOTS + c)
                    if e == 0:
                        dve.wait_ge(acc_free, b + 1)
                    if e == E - 1:
                        route(b + 1, 0)
                    for t in range(BLK):
                        add_expert(b * E + e, e, t, e == 0)
                        attend(2 * b + (half + 2), half, k * SLOTS + FC + t)
                        if e == E - 1:
                            route(b + 1, t + 1)
                finish(b)
                take_gates(b + 1)
            for c in range(FC):
                expert_up((NBLK - 1) * E, c)
            dve.wait_ge(x2_biased, NBLK)
            dve.wait_ge(gates_taken, NBLK)
            dve.wait_ge(acc_free, NBLK)
            for t in range(BLK):
                add_expert((NBLK - 1) * E, 0, t, True)
            with dve.Fori(1, E) as e:
                for c in range(FC):
                    expert_up(e + (NBLK - 1) * E, c)
                for t in range(BLK):
                    add_expert(e + (NBLK - 1) * E, e, t)
            finish(NBLK - 1)

        @block.gpsimd
        def _(pool):
            def root(which, tiles, step, eps_done, rstd_done, base):
                pool.wait_ge(step, 2 * base + 2)
                nc.gpsimd.tensor_tensor(var_eps[:, which, 0:tiles], moments[:, which, 0:tiles, 1], eps_row[:, 0:tiles],
                                        ALU.add).then_inc(eps_done, 1)
                pool.wait_ge(eps_done, base + 1)
                nc.gpsimd.tensor_tensor(rstd[:, which, 0:tiles], var_eps[:, which, 0:tiles], power[:, 0:tiles],
                                        ALU.pow).then_inc(rstd_done, 1)

            def attend(p, s):
                if s == X_STEP:
                    pool.wait_ge(x_loaded, 16 * (p + 1))
                    if not first(p):
                        pool.wait_ge(y1_sum, p)
                    for j in range(PAIR):
                        i = nc.gpsimd.tensor_tensor(x_bo[:, j], x_in[:, j], bo_all[:], ALU.add)
                    i.then_inc(x_bo_ready, 1)
                if s == WO_STEP:
                    root(0, PAIR, ln1_step, ln1_eps, ln1_rstd, p)
                if s == REC_STEP:
                    pool.wait_ge(xa_step, 6 * p + 2)
                    pool.wait_ge(exps_ready, p + 1)
                    nc.gpsimd.tensor_tensor(y1t[:], y1t[:], scan_a[:], ALU.add).then_inc(mix_a_ready, 1)
                if s == BACK_STEP:
                    root(1, PAIR, ln2_step, ln2_eps, ln2_rstd, p)

            def low(dst, src, hi, i):
                cols = slice(i * PW, (i + 1) * PW)
                return nc.gpsimd.tensor_tensor(dst[:, cols], src[:, cols], hi[:, cols].bitcast(F32), ALU.subtract)

            def split_w2(n, i):
                pool.wait_ge(w2_hi_ready, PIECES * n + (i + 1))
                low(w2_lo, w2_raw, w2_hi, i).then_inc(w2_ready, 1)

            def split_w1(n, i):
                pool.wait_ge(w1_hi_ready, PIECES * n + (i + 1))
                low(w1_lo, w1_raw, w1_hi, i).then_inc(w1_ready, 1)

            def finish(b):
                root(2, BLK, ln3_step, ln3_eps, ln3_rstd, b)
                pool.wait_ge(out_ready, b + 1)
                pool.dma_start(out[bass.ds(BLK * b, BLK)].rearrange("j s d -> s j d"), acc[:]).then_inc(stored, 16)
                pool.wait_ge(stored, 16 * (b + 1))
                pool.sem_inc(acc_free, 1)

            pool.sem_inc(acc_free, 1)
            nc.gpsimd.memset(ident[:], 0.0).then_inc(masks_made, 1)
            nc.gpsimd.memset(head_mask[:], 1.0).then_inc(masks_made, 1)
            nc.gpsimd.memset(power[:], -0.5)
            nc.gpsimd.memset(eps_row[:], EPS).then_inc(masks_made, 1)
            pool.wait_ge(masks_made, 3)
            nc.gpsimd.affine_select(out=ident[:], in_=ident[:], compare_op=ALU.not_equal, fill=1.0,
                                    base=0, pattern=[[-1, P]], channel_multiplier=1).then_inc(masks_made, 1)
            nc.gpsimd.affine_select(out=head_mask[:], in_=head_mask[:], compare_op=ALU.is_ge, fill=0.0,
                                    base=0, pattern=[[-DH, HC]], channel_multiplier=1).then_inc(masks_made, 1)
            pool.wait_ge(masks_made, 5)
            nc.gpsimd.affine_select(out=head_mask[:], in_=head_mask[:], compare_op=ALU.is_ge, fill=0.0,
                                    base=DH - 1, pattern=[[DH, HC]], channel_multiplier=-1).then_inc(masks_made, 1)
            pool.wait_ge(consts_loaded, 16 * CONSTS)
            for i in range(PIECES):
                split_w1(0, i)
            for p, s in ALONE:
                attend(p, s)
            with pool.Fori(0, NBLK - 1) as b:
                for e in range(E):
                    half, k = divmod(e, SC)
                    for c in range(FC):
                        if c < PIECES:
                            split_w2(b * E + e, c)
                        attend(2 * b + (half + 2), k * SLOTS + c)
                    for t in range(BLK):
                        if t < PIECES // 2:
                            split_w1(b * E + (e + 1), 2 * t)
                            split_w1(b * E + (e + 1), 2 * t + 1)
                        attend(2 * b + (half + 2), k * SLOTS + FC + t)
                finish(b)
            with pool.Fori(0, E - 1) as e:
                for i in range(PIECES):
                    split_w2(e + (NBLK - 1) * E, i)
                for i in range(PIECES):
                    split_w1(e + ((NBLK - 1) * E + 1), i)
            for i in range(PIECES):
                split_w2(NBLK * E - 1, i)
            finish(NBLK - 1)


X_STEP, QK_STEP, V_STEP, VSPLIT_STEP = 0, 2, 3, 9
SCORE_STEP = [7, 8, 18, 19]
EXP_STEP = [8, 9, 20, 21]
TURN_STEP = [10, 13, 22, 24]
VALUE_STEP = [11, 15, 23, 26]
ATT_STEP, CTX_STEP, WO_STEP, NORM1_STEP, Y1_STEP = 28, 29, 30, 32, 32
XEXP_STEP, REC_STEP, BACK_STEP, NORM2_STEP = 33, 34, 40, 41
ALONE = ([(0, s) for s in range(X_STEP, WO_STEP + 1)]
         + [(1, s) for s in range(X_STEP, V_STEP + 1)]
         + [(0, s) for s in range(WO_STEP + 1, REC_STEP + 1)]
         + [(1, s) for s in range(V_STEP + 1, SCORE_STEP[0] + 1)]
         + [(0, s) for s in range(REC_STEP + 1, NORM2_STEP + 1)]
         + [(1, s) for s in range(SCORE_STEP[0] + 1, NORM2_STEP + 1)])
ROUTE_PARTS = 5
MASKS = 6
DVE_SETUP = 4


def kernel(**inputs):
    import numpy as _np
    import concourse.bacc as _bacc
    from concourse.bass_utils import run_bass_kernel_spmd as _run

    a = {k.replace("L0_", ""): _np.asarray(v) for k, v in inputs.items()}
    D = a["x"].shape[2]
    E, F = a["ffn_b1"].shape
    by_in = lambda w: w.transpose(1, 0, 2).reshape(D, D)
    laid = {
        "x": a["x"], "ctx": a["ctx_1024"],
        "wq": by_in(a["attn_wq"]), "wk": by_in(a["attn_wk"]), "wv": by_in(a["attn_wv"]), "wo": a["attn_wo"].T,
        "cols": _np.stack([a[k].reshape(D // 128, 128).T for k in ("attn_bq", "attn_bk", "xattn_w", "xattn_u")], axis=1),
        "bv": a["attn_bv"].reshape(D), "bo": a["attn_bo"],
        "wg": a["ffn_Wg"].T.reshape(D // 128, 128, E),
        "w1": a["ffn_W1"],
        "b1": a["ffn_b1"].reshape(E, F // 128, 128).transpose(2, 0, 1).reshape(128, E * F // 128),
        "w2": a["ffn_W2"], "b2": a["ffn_b2"],
    }
    nc = _bacc.Bacc("TRN2", target_bir_lowering=False, num_devices=1)
    arrays, args = {}, []
    for name, v in laid.items():
        arrays[f"in_{name}_dram"] = _np.ascontiguousarray(v)
        args.append(nc.dram_tensor(f"in_{name}_dram", v.shape, mybir.dt.from_np(v.dtype), kind="ExternalInput").ap())
    out = nc.dram_tensor("out_dram", a["x"].shape, F32, kind="ExternalOutput").ap()
    decoder_layer(nc, *args, out)
    return _run(nc, [arrays], core_ids=[0]).results[0]["out_dram"]
```

```python
from contextlib import ExitStack

import concourse.bass as bass
from concourse import mybir

F32 = mybir.dt.float32
F32R = mybir.dt.float32r
F16 = mybir.dt.float16
BF16 = mybir.dt.bfloat16
ALU = mybir.AluOpType
ACT = mybir.ActivationFunctionType
AX_X = mybir.AxisListType.X

P = 128
EPS = 1e-5


def decoder_layer(nc, x, ctx_in, wq, wk, wv, wo, cols, bv, bo, wg, w1, b1, w2, b2, out):
    B, S, D = x.shape
    E, _, F = w1.shape
    H = 16
    DH = D // H
    C = D // P
    HC = H // C
    HQ = HC // 2
    FC = F // P
    G = FC // 2
    PAIR = 2
    NPAIR = B // PAIR
    TOK = PAIR * S
    BOTH = 2 * TOK
    VW = DH + 1
    QUADS = PAIR * C * 2
    UNITS = PAIR * C
    SLOTS = 2 * G
    PW = C * F // G
    assert S == P and C == 2 and DH == 16 and BOTH == 512 and NPAIR * PAIR == B
    assert SLOTS * E > ROUTE_STEP[-1] and E % 2 == 0

    with ExitStack() as ctx:
        def sb(name, shape, dt=F32):
            return ctx.enter_context(nc.sbuf_tensor(name, shape, dt))

        def sem(name):
            return ctx.enter_context(nc.semaphore(name))

        ident = sb("ident", [P, P])
        head_mask = sb("head_mask", [P, HC])
        ramp = sb("ramp", [P, S])
        ones = sb("ones", [P, S])
        proj_hi = sb("proj_hi", [P, 4, C, D], F32R)
        proj_lo = sb("proj_lo", [P, 4, C, D], F32R)
        bqk = sb("bqk", [P, 2, C])
        bq_scaled = sb("bq_scaled", [P, C])
        bv_all = sb("bv_all", [P, D])
        bo_all = sb("bo_all", [P, D])
        wu = sb("wu", [P, 2, C])
        decay = sb("decay", [P, 2, C])
        decay_row = sb("decay_row", [P, 2, C, S])
        wg_raw = sb("wg_raw", [P, C, E])
        wg_hi = sb("wg_hi", [P, C, P], F32R)
        wg_lo = sb("wg_lo", [P, C, P], F32R)
        b1_all = sb("b1_all", [P, E * FC])
        b2_raw = sb("b2_raw", [E, D])
        b2_hi = sb("b2_hi", [E, D], F32R)
        b2_lo = sb("b2_lo", [E, D], F32R)
        power = sb("power", [P, PAIR])
        eps_row = sb("eps_row", [P, PAIR])

        x_in = sb("x_in", [P, PAIR, D])
        ctx_sb = sb("ctx_sb", [P, PAIR, D])
        x_bo = sb("x_bo", [P, PAIR, D])
        xt_hi = sb("xt_hi", [P, C, PAIR * S], F32R)
        xt_lo = sb("xt_lo", [P, C, PAIR * S], F32R)
        q_all = sb("q_all", [P, C, PAIR * S])
        q_hi = sb("q_hi", [P, C, PAIR * S], F32R)
        q_lo = sb("q_lo", [P, C, PAIR * S], F32R)
        k_both = sb("k_both", [P, 2, C, PAIR * S])
        k_hi = sb("k_hi", [P, C, PAIR * S], F32R)
        kd = sb("kd", [P, 2, PAIR, HC, S], F32R)
        v_all = sb("v_all", [P, PAIR, D])
        v_hi = sb("v_hi", [P, PAIR, H, VW], BF16)
        v_mid = sb("v_mid", [P, PAIR, H, VW], BF16)
        v_lo = sb("v_lo", [P, PAIR, H, VW], BF16)
        neg_max = sb("neg_max", [P, QUADS, HQ])
        probs = sb("probs", [P, 2, 2, HQ, S])
        pt_hi = sb("pt_hi", [P, 2, HQ, S], F16)
        pt_lo = sb("pt_lo", [P, 2, HQ, S], F16)
        inv_sum = sb("inv_sum", [P, UNITS, HC])
        att = sb("att", [P, PAIR, D])
        y1 = sb("y1", [P, PAIR, D])
        stats = sb("stats", [P, PAIR, 6])
        moments = sb("moments", [P, 3, PAIR, 2])
        spare = sb("spare", [P, 3])
        var_eps = sb("var_eps", [P, 3, PAIR])
        rstd = sb("rstd", [P, 3, PAIR])
        y1t = sb("y1t", [P, C, PAIR, S])
        ctx_t = sb("ctx_t", [P, C, PAIR, S])
        exp_k = sb("exp_k", [P, C, PAIR, S])
        exp_uk = sb("exp_uk", [P, C, PAIR, S])
        inc_a = sb("inc_a", [P, C, PAIR, S])
        inc_b = sb("inc_b", [P, C, PAIR, S])
        x2 = sb("x2", [P, PAIR, D])

        next_hi = sb("next_hi", [P, C, TOK], F32R)
        next_lo = sb("next_lo", [P, C, TOK], F32R)
        x2t_hi = sb("x2t_hi", [P, C, TOK], F32R)
        x2t_lo = sb("x2t_lo", [P, C, TOK], F32R)
        logits = sb("logits", [P, PAIR, E])
        gate_t_hi = sb("gate_t_hi", [E, TOK], F32R)
        gate_t_lo = sb("gate_t_lo", [E, TOK], F32R)
        route_exps = sb("route_exps", [P, PAIR, E])
        route_max = sb("route_max", [P, PAIR])
        route_sum = sb("route_sum", [P, PAIR])
        route_inv = sb("route_inv", [P, PAIR])
        next_gate = sb("next_gate", [P, PAIR, E])
        gate = sb("gate", [P, PAIR, E])
        w1_raw = sb("w1_raw", [P, 2, C * F])
        w2_raw = sb("w2_raw", [P, 2, C * F])
        w1_hi = sb("w1_hi", [P, C * F], F32R)
        w1_lo = sb("w1_lo", [P, C * F], F32R)
        w2_hi = sb("w2_hi", [P, C * F], F32R)
        w2_lo = sb("w2_lo", [P, C * F], F32R)
        h_all = sb("h_all", [P, G, BOTH])
        h_hi = sb("h_hi", [P, G, BOTH], F32R)
        h_lo = sb("h_lo", [P, G, BOTH], F32R)
        acc = sb("acc", [P, PAIR, D])

        projections = w2_raw[:, 1].rearrange("p (i c d) -> p i c d", i=4, c=C)
        w1h = w1_hi[:].rearrange("p (c f) -> p c f", c=C)
        w1l = w1_lo[:].rearrange("p (c f) -> p c f", c=C)
        w2h = w2_hi[:].rearrange("p (c d) -> p c d", c=FC)
        w2l = w2_lo[:].rearrange("p (c d) -> p c d", c=FC)
        logits_t = exp_uk[:].rearrange("p c j t -> p (c j t)")[:, 0:TOK]
        scan_a, scan_b = inc_a, inc_b
        mix = exp_k[:]

        up_ps = [ctx.enter_context(nc.psum_tensor(f"up_ps{i}", [P, BOTH], F32)) for i in range(2)]
        down_ps = [ctx.enter_context(nc.psum_tensor(f"down_ps{i}", [P, 512], F32)) for i in range(2)]
        bank = [ctx.enter_context(nc.psum_tensor(f"bank{i}", [P, 512], F32)) for i in range(4)]

        def group(w, g):
            return w.rearrange("p (c f) -> p c f", c=C)[:, :, g * F // G:(g + 1) * F // G]

        def by_chunk(t):
            return t[:].rearrange("p (c n) -> p c n", c=C)

        def by_head(t):
            return t[:].rearrange("p (h t) -> p h t", h=HQ)

        def by_tile(t):
            return t[:].rearrange("p (j d) -> p j d", j=PAIR)

        def by_cjt(t):
            return t[:].rearrange("p (c j t) -> p c j t", c=C, j=PAIR)

        consts_loaded = sem("consts_loaded")
        masks_made = sem("masks_made")
        proj_loaded = [sem(f"proj_loaded{i}") for i in range(2)]
        proj_hi_ready = sem("proj_hi_ready")
        proj_ready = sem("proj_ready")
        decay_ready = sem("decay_ready")
        dve_setup = sem("dve_setup")
        act_setup = sem("act_setup")
        x_loaded = sem("x_loaded")
        ctx_loaded = sem("ctx_loaded")
        xt_ps = sem("xt_ps")
        xt_hi_ready = sem("xt_hi_ready")
        xt_ready = sem("xt_ready")
        q_ps = sem("q_ps")
        k_ps = sem("k_ps")
        v_ps = sem("v_ps")
        q_hi_ready = sem("q_hi_ready")
        q_ready = sem("q_ready")
        k_hi_ready = sem("k_hi_ready")
        k_rest_ready = sem("k_rest_ready")
        kd_ready = sem("kd_ready")
        first_keys_ready = sem("first_keys_ready")
        v_step = sem("v_step")
        scores_ps = sem("scores_ps")
        max_ready = sem("max_ready")
        shifted = sem("shifted")
        probs_ready = sem("probs_ready")
        pt_ps = sem("pt_ps")
        pt_hi_ready = sem("pt_hi_ready")
        pt_ready = sem("pt_ready")
        pv_ps = sem("pv_ps")
        inv_ready = sem("inv_ready")
        att_ready = sem("att_ready")
        att_t_ps = sem("att_t_ps")
        att_hi_ready = sem("att_hi_ready")
        att_t_ready = sem("att_t_ready")
        wo_ps = sem("wo_ps")
        x_bo_ready = sem("x_bo_ready")
        y1_sum = sem("y1_sum")
        ln1_step = sem("ln1_step")
        ln1_eps = sem("ln1_eps")
        ln1_rstd = sem("ln1_rstd")
        y1_ready = sem("y1_ready")
        ctx_t_ps = sem("ctx_t_ps")
        ctx_t_ready = sem("ctx_t_ready")
        y1t_ps = sem("y1t_ps")
        exp_minus_ready = sem("exp_minus_ready")
        exps_ready = sem("exps_ready")
        xa_step = sem("xa_step")
        mix_a_ready = sem("mix_a_ready")
        mix_ready = sem("mix_ready")
        x2_ps = sem("x2_ps")
        ln2_step = sem("ln2_step")
        ln2_eps = sem("ln2_eps")
        ln2_rstd = sem("ln2_rstd")
        x2_ready = sem("x2_ready")
        x2t_ps = sem("x2t_ps")
        x2t_hi_ready = sem("x2t_hi_ready")
        x2t_ready = sem("x2t_ready")
        x2t_moved = sem("x2t_moved")
        logits_t_ps = sem("logits_t_ps")
        logits_t_ready = sem("logits_t_ready")
        logits_ps = sem("logits_ps")
        route_step = sem("route_step")
        route_exp = sem("route_exp")
        gate_ready = sem("gate_ready")
        gates_taken = sem("gates_taken")
        gate_t_ps = sem("gate_t_ps")
        gate_hi_ready = sem("gate_hi_ready")
        gate_t_ready = sem("gate_t_ready")
        b2_ps = sem("b2_ps")
        stored = sem("stored")
        acc_free = sem("acc_free")
        x2_biased = sem("x2_biased")
        ln3_step = sem("ln3_step")
        ln3_eps = sem("ln3_eps")
        ln3_rstd = sem("ln3_rstd")
        out_ready = sem("out_ready")
        w1_loaded = [sem(f"w1_loaded{i}") for i in range(2)]
        w2_loaded = [sem(f"w2_loaded{i}") for i in range(2)]
        w1_hi_ready = sem("w1_hi_ready")
        w1_ready = sem("w1_ready")
        w2_hi_ready = sem("w2_hi_ready")
        w2_ready = sem("w2_ready")
        up_done = sem("up_done")
        gelu_done = sem("gelu_done")
        h_hi_ready = sem("h_hi_ready")
        h_ready = sem("h_ready")
        down_done = sem("down_done")
        added = sem("added")

        CONSTS = 8

        def first(p):
            return isinstance(p, int) and p == 0

        def score_banks(p, u):
            return (bank, up_ps, down_ps, up_ps)[u] if first(p) else bank

        first_keys = [t[:].rearrange("p g (a t) -> p (g a) t", t=S).rearrange("p (j h) t -> p j h t", j=PAIR)
                      for t in (h_hi, h_lo)]

        def keys(p, c, j, heads):
            if first(p) and c == 1:
                return [t[:, j, heads, :] for t in first_keys]
            return kd[:, 0, j, heads, :], kd[:, 1, j, heads, :]

        def values_by_head(t):
            return t[:].rearrange("p j (h e) -> p j h e", h=H)

        block = ctx.enter_context(nc.Block())


        @block.sync
        def _(sp):
            def load_pair(p):
                sp.wait_ge(xt_ps, p)
                sp.wait_ge(x_bo_ready, p)
                sp.dma_start(x_in[:], x[bass.ds(PAIR * p, PAIR)].rearrange("j s d -> s j d")).then_inc(x_loaded, 16)
                sp.wait_ge(ctx_t_ps, p)
                sp.dma_start(ctx_sb[:], ctx_in[bass.ds(PAIR * p, PAIR)].rearrange("j s d -> s j d")).then_inc(ctx_loaded, 16)

            def load_w1(e, n, parity, reused=True):
                if reused:
                    sp.wait_ge(w1_ready, G * (n - 1))
                w = w1[e] if isinstance(e, int) else w1[bass.ds(e, 1)].rearrange("a r f -> (a r) f")
                sp.dma_start(w1_raw[:, parity].rearrange("p (c f) -> p c f", c=C), w.rearrange("(c p) f -> p c f", p=P))\
                    .then_inc(w1_loaded[parity], 16)

            def load_w2(e, n, parity, reused=True):
                if reused:
                    sp.wait_ge(w2_ready, G * (n - 1))
                w = w2[e] if isinstance(e, int) else w2[bass.ds(e, 1)].rearrange("a r d -> (a r) d")
                sp.dma_start(w2_raw[:, parity].rearrange("p (c d) -> p c d", c=FC), w.rearrange("(c p) d -> p c d", p=P))\
                    .then_inc(w2_loaded[parity], 16)

            def store(b):
                sp.wait_ge(out_ready, b + 1)
                sp.dma_start(out[bass.ds(PAIR * b, PAIR)].rearrange("j s d -> s j d"), acc[:]).then_inc(stored, 16)
                sp.wait_ge(stored, 16 * (b + 1))
                sp.sem_inc(acc_free, 1)

            sp.sem_inc(acc_free, 1)
            sp.dma_start(x_in[:], x[0:PAIR].rearrange("j s d -> s j d")).then_inc(x_loaded, 16)
            for i, w in enumerate((wq, wk, wv, wo)):
                sp.dma_start(projections[:, i], w.rearrange("(c p) d -> p c d", p=P)).then_inc(proj_loaded[i // 2], 16)
            sp.dma_start(bqk[:], cols[:, 0:2, :]).then_inc(consts_loaded, 16)
            sp.dma_start(wu[:], cols[:, 2:4, :]).then_inc(consts_loaded, 16)
            sp.dma_start(bv_all[:], bv.rearrange("(a d) -> a d", a=1).to_broadcast([P, D])).then_inc(consts_loaded, 16)
            sp.dma_start(bo_all[:], bo.rearrange("(a d) -> a d", a=1).to_broadcast([P, D])).then_inc(consts_loaded, 16)
            for c in range(C):
                sp.dma_start(wg_raw[:, c, :], wg[c]).then_inc(consts_loaded, 16)
            sp.dma_start(b1_all[:], b1).then_inc(consts_loaded, 16)
            sp.dma_start(b2_raw[:], b2).then_inc(consts_loaded, 16)
            sp.dma_start(ctx_sb[:], ctx_in[0:PAIR].rearrange("j s d -> s j d")).then_inc(ctx_loaded, 16)
            load_w1(0, 0, 0, reused=False)
            load_w2(0, 0, 0, reused=False)
            load_w1(1, 1, 1, reused=False)
            sp.wait_ge(proj_ready, 4)
            load_w2(1, 1, 1, reused=False)

            load_pair(1)

            def load_weights(b):
                for e in range(E):
                    load_w1((e + 2) % E, b * E + (e + 2), e % 2)
                    load_w2((e + 2) % E, b * E + (e + 2), e % 2)

            with sp.Fori(0, NPAIR - 2) as b:
                load_weights(b)
                load_pair(b + 2)
                store(b)
            load_weights(NPAIR - 2)
            store(NPAIR - 2)
            with sp.Fori(0, E // 2 - 1) as k:
                for j in range(2):
                    load_w1(k * 2 + (j + 2), k * 2 + ((NPAIR - 1) * E + j + 2), j)
                    load_w2(k * 2 + (j + 2), k * 2 + ((NPAIR - 1) * E + j + 2), j)
            store(NPAIR - 1)

        @block.tensor
        def _(pe):
            def product(ps, hi, lo, rhs_hi, rhs_lo, first=True, last=True):
                nc.tensor.matmul(ps, hi, rhs_hi, start=first, stop=False)
                nc.tensor.matmul(ps, hi, rhs_lo, start=False, stop=False)
                return nc.tensor.matmul(ps, lo, rhs_hi, start=False, stop=last)

            def project(ps, which, c):
                for kc in range(C):
                    cols = slice(c * P, (c + 1) * P)
                    mm = product(ps, proj_hi[:, which, kc, cols], proj_lo[:, which, kc, cols],
                                 xt_hi[:, kc, :], xt_lo[:, kc, :], kc == 0, kc == C - 1)
                return mm

            def project_rows(ps, which, j):
                for kc in range(C):
                    rows = slice(j * S, (j + 1) * S)
                    mm = product(ps, xt_hi[:, kc, rows], xt_lo[:, kc, rows],
                                 proj_hi[:, which, kc, :], proj_lo[:, which, kc, :], kc == 0, kc == C - 1)
                return mm

            def turn(dst, src):
                for c in range(C):
                    for j in range(PAIR):
                        mm = nc.tensor.transpose(dst[:, c, j * S:(j + 1) * S], src[:, j, c * P:(c + 1) * P], ident[:])
                return mm

            def scores(p, u):
                c, j = divmod(u, PAIR)
                if first(p) and u == 2:
                    pe.wait_ge(first_keys_ready, 1)
                rows = slice(j * S, (j + 1) * S)
                if u == 2 and not first(p):
                    pe.wait_ge(att_ready, UNITS * p + 2)
                for i in range(2):
                    if u == 0 or u == 2 and not first(p):
                        pe.wait_ge(kd_ready, i + 1 if first(p) else 2 * C * p + (2 * c + i - 1))
                    if u % 2 and not first(p):
                        pe.wait_ge(shifted, QUADS * p + (2 * u - 1 + i))
                    if u == 3 and first(p):
                        pe.wait_ge(shifted, 3 + i)
                    keys_hi, keys_lo = keys(p, c, j, slice(i * HQ, (i + 1) * HQ))
                    product(by_head(score_banks(p, u)[i]), q_hi[:, c, rows], q_lo[:, c, rows],
                            keys_hi, keys_lo).then_inc(scores_ps, 1)

            def turn_probs(p, u):
                if u == 0 and not first(p):
                    pe.wait_ge(x2_ready, p)
                for i in range(2):
                    g = 2 * u + i
                    pe.wait_ge(probs_ready, QUADS * p + (g + 1))
                    for h in range(HQ):
                        mm = nc.tensor.transpose(by_head(bank[2 + i])[:, h, :], probs[:, u % 2, i, h, :], ident[:])
                    mm.then_inc(pt_ps, 1)

            def weigh_values(p, u):
                c, j = divmod(u, PAIR)
                if u == 0:
                    pe.wait_ge(v_step, 5 * (p + 1))
                if u % 2 == 0 and not first(p):
                    pe.wait_ge(shifted, QUADS * p + (2 * u + 4))
                if first(p) and u < 2:
                    pe.wait_ge(shifted, 2)
                if first(p) and u >= 2:
                    pe.wait_ge(att_ready, u - 1)
                for i in range(2):
                    pe.wait_ge(pt_ready, QUADS * p + (2 * u + i + 1))
                    for h in range(HQ):
                        slot = i * HQ + h
                        ps = bank[u % 2][:, slot * VW:(slot + 1) * VW]
                        head = c * HC + i * HQ + h
                        hi, lo = pt_hi[:, i, h, :], pt_lo[:, i, h, :]
                        nc.tensor.matmul(ps, hi, v_hi[:, j, head, :], start=True, stop=False)
                        nc.tensor.matmul(ps, hi, v_mid[:, j, head, :], start=False, stop=False)
                        nc.tensor.matmul(ps, hi, v_lo[:, j, head, :], start=False, stop=False)
                        nc.tensor.matmul(ps, lo, v_hi[:, j, head, :], start=False, stop=False)
                        mm = nc.tensor.matmul(ps, lo, v_mid[:, j, head, :], start=False, stop=True)
                    mm.then_inc(pv_ps, 1)

            def attend(p, s):
                if s == X_STEP:
                    pe.wait_ge(x_loaded, 16 * (p + 1))
                    turn(by_chunk(bank[0]), x_in).then_inc(xt_ps, 1)
                if s == QK_STEP:
                    if first(p):
                        pe.wait_ge(proj_ready, 2)
                    else:
                        pe.wait_ge(ctx_t_ready, p)
                    pe.wait_ge(xt_ready, p + 1)
                    project(by_chunk(bank[2])[:, 0, :], 1, 0)
                    project(by_chunk(bank[2])[:, 1, :], 1, 1).then_inc(k_ps, 1)
                    project(by_chunk(bank[1])[:, 0, :], 0, 0)
                    project(by_chunk(bank[1])[:, 1, :], 0, 1).then_inc(q_ps, 1)
                if s == V_STEP:
                    if first(p):
                        pe.wait_ge(proj_ready, 4)
                    else:
                        pe.wait_ge(x2_biased, p)
                    project_rows(by_tile(bank[3])[:, 0, :], 2, 0)
                    project_rows(by_tile(bank[3])[:, 1, :], 2, 1).then_inc(v_ps, 1)
                if s == SCORE_STEP[0]:
                    pe.wait_ge(q_ready, p + 1)
                    if not first(p):
                        pe.wait_ge(exps_ready, p)
                for u in range(UNITS):
                    if s == SCORE_STEP[u]:
                        scores(p, u)
                    if s == TURN_STEP[u]:
                        turn_probs(p, u)
                    if s == VALUE_STEP[u]:
                        weigh_values(p, u)
                if s == ATT_STEP:
                    pe.wait_ge(att_ready, UNITS * (p + 1))
                    turn(by_chunk(bank[2]), att).then_inc(att_t_ps, 1)
                if s == WO_STEP:
                    pe.wait_ge(att_t_ready, p + 1)
                    project_rows(by_tile(bank[3])[:, 0, :], 3, 0)
                    project_rows(by_tile(bank[3])[:, 1, :], 3, 1).then_inc(wo_ps, 1)
                if s == CTX_STEP:
                    pe.wait_ge(ctx_loaded, 16 * (p + 1))
                    turn(by_chunk(bank[1]), ctx_sb).then_inc(ctx_t_ps, 1)
                if s == Y1_STEP:
                    pe.wait_ge(y1_ready, p + 1)
                    turn(by_chunk(bank[0]), y1).then_inc(y1t_ps, 1)
                if s == BACK_STEP:
                    pe.wait_ge(mix_ready, p + 1)
                    for j in range(PAIR):
                        for c in range(C):
                            mm = nc.tensor.transpose(by_tile(bank[2])[:, j, c * P:(c + 1) * P], mix[:, c, j, :], ident[:])
                    mm.then_inc(x2_ps, 1)

            def route(b, part):
                if part == 0:
                    pe.wait_ge(x2_ready, b + 1)
                    for c in range(C):
                        for t in range(PAIR):
                            mm = nc.tensor.transpose(bank[c][:, t * S:(t + 1) * S], x2[:, t, c * P:(c + 1) * P], ident[:])
                        mm.then_inc(x2t_ps, 1)
                if part == 1:
                    if first(b):
                        pe.wait_ge(dve_setup, DVE_SETUP)
                    pe.wait_ge(x2t_ready, C * (b + 1))
                    for kc in range(C):
                        mm = product(bank[2][:, 0:TOK], wg_hi[:, kc, :], wg_lo[:, kc, :],
                                     next_hi[:, kc, :], next_lo[:, kc, :], kc == 0, kc == C - 1)
                    mm.then_inc(logits_t_ps, 1)
                if part == 2:
                    pe.wait_ge(logits_t_ready, b + 1)
                    for t in range(PAIR):
                        mm = nc.tensor.transpose(bank[3][:, t * P:(t + 1) * P], logits_t[:, t * S:(t + 1) * S], ident[:])
                    mm.then_inc(logits_ps, 1)
                if part == 4:
                    pe.wait_ge(gate_ready, b + 1)
                    for t in range(PAIR):
                        mm = nc.tensor.transpose(bank[2][0:E, t * S:(t + 1) * S], next_gate[:, t, :], ident[:])
                    mm.then_inc(gate_t_ps, 1)
                if part == 5:
                    pe.wait_ge(gate_t_ready, b + 1)
                    for t in range(PAIR):
                        rows = slice(t * S, (t + 1) * S)
                        mm = product(by_tile(bank[3])[:, t, :], gate_t_hi[:, rows], gate_t_lo[:, rows], b2_hi[:], b2_lo[:])
                    mm.then_inc(b2_ps, 1)

            def up(n, g):
                pe.wait_ge(w1_ready, G * n + (g + 1))
                if g >= 2:
                    pe.wait_ge(gelu_done, G * n + (g - 1))
                for k in range(2):
                    cols = slice((2 * g + k) * P, (2 * g + k + 1) * P)
                    for kc in range(C):
                        mm = product(up_ps[g % 2][:, k * TOK:(k + 1) * TOK], w1h[:, kc, cols], w1l[:, kc, cols],
                                     x2t_hi[:, kc, :], x2t_lo[:, kc, :], kc == 0, kc == C - 1)
                mm.then_inc(up_done, 1)

            def down(n, g):
                pe.wait_ge(w2_ready, G * n + (g + 1))
                pe.wait_ge(h_ready, G * n + (g + 1))
                for k in range(2):
                    c = 2 * g + k
                    for t in range(PAIR):
                        cols = slice(k * TOK + t * S, k * TOK + (t + 1) * S)
                        mm = product(down_ps[t][:, 0:D], h_hi[:, g, cols], h_lo[:, g, cols],
                                     w2h[:, c, :], w2l[:, c, :], c == 0, c == FC - 1)
                        if c == FC - 1:
                            mm.then_inc(down_done, 1)

            def expert(n, g):
                if g < G:
                    up(n, g)
                else:
                    down(n, g - G)

            pe.wait_ge(masks_made, MASKS)
            for s in FIRST_ORDER:
                attend(0, s)
                if s in ROUTE_STEP:
                    route(0, ROUTE_STEP.index(s))
            with pe.Fori(0, NPAIR - 1) as b:
                pe.wait_ge(x2t_moved, b * 2 + 2)
                for e in range(E):
                    for g in range(SLOTS):
                        s = e * SLOTS + g
                        expert(b * E + e, g)
                        if s in GATE_STEP:
                            route(b, 4 + GATE_STEP.index(s))
                        attend(b + 1, s)
                        if s in ROUTE_STEP:
                            route(b + 1, ROUTE_STEP.index(s))
            pe.wait_ge(x2t_moved, 2 * NPAIR)
            for g in range(SLOTS):
                expert((NPAIR - 1) * E, g)
                if g in GATE_STEP:
                    route(NPAIR - 1, 4 + GATE_STEP.index(g))
            with pe.Fori(1, E) as e:
                for g in range(SLOTS):
                    expert(e + (NPAIR - 1) * E, g)

        @block.scalar
        def _(act):
            def attend(p, s):
                if s == X_STEP:
                    act.wait_ge(xt_ps, p + 1)
                    nc.scalar.activation(xt_hi[:], by_chunk(bank[0]), ACT.Copy).then_inc(xt_hi_ready, 1)
                if s == QK_STEP:
                    act.wait_ge(k_ps, p + 1)
                    for dst in (k_both[:, 0], k_hi):
                        for c in range(C):
                            a = nc.scalar.activation(dst[:, c, :], by_chunk(bank[2])[:, c, :], ACT.Identity,
                                                     bias=bqk[:, 1, c:c + 1])
                    a.then_inc(k_hi_ready, 1)
                    act.wait_ge(q_ps, p + 1)
                    for dst in (q_all, q_hi):
                        for c in range(C):
                            a = nc.scalar.activation(dst[:, c, :], by_chunk(bank[1])[:, c, :], ACT.Identity,
                                                     bias=bq_scaled[:, c:c + 1], scale=DH ** -0.5)
                    a.then_inc(q_hi_ready, 1)
                    if first(p):
                        act.wait_ge(masks_made, MASKS)
                        act.wait_ge(k_rest_ready, 1)
                        for h in range(HC):
                            for part, t in enumerate(first_keys):
                                a = nc.scalar.activation(t[:, :, h, :], k_both[:, part, 1, :].rearrange("p (j t) -> p j t", j=PAIR),
                                                         ACT.Copy, scale=head_mask[:, h:h + 1])
                        a.then_inc(first_keys_ready, 1)
                for u in range(UNITS):
                    if s == EXP_STEP[u]:
                        for i in range(2):
                            act.wait_ge(shifted, QUADS * p + (2 * u + i + 1))
                            nc.scalar.activation(probs[:, u % 2, i], probs[:, u % 2, i], ACT.Exp).then_inc(probs_ready, 1)
                    if s == TURN_STEP[u]:
                        for i in range(2):
                            g = 2 * u + i
                            act.wait_ge(pt_ps, QUADS * p + (g + 1))
                            if u > 0:
                                act.wait_ge(pv_ps, QUADS * p + (g - 1))
                            nc.scalar.activation(pt_hi[:, i], by_head(bank[2 + i]), ACT.Copy).then_inc(pt_hi_ready, 1)
                if s == ATT_STEP:
                    act.wait_ge(att_t_ps, p + 1)
                    nc.scalar.activation(xt_hi[:], by_chunk(bank[2]), ACT.Copy).then_inc(att_hi_ready, 1)
                if s == CTX_STEP:
                    act.wait_ge(ctx_t_ps, p + 1)
                    nc.scalar.activation(ctx_t[:], by_cjt(bank[1]), ACT.Copy).then_inc(ctx_t_ready, 1)
                if s == XEXP_STEP:
                    act.wait_ge(y1t_ps, p + 1)
                    k = by_cjt(bank[0])
                    nc.scalar.activation(inc_b[:, :, :, 2:S], k[:, :, :, 1:S - 1], ACT.Exp, scale=-1.0).then_inc(exp_minus_ready, 1)
                    nc.scalar.activation(exp_k[:], k, ACT.Exp)
                    for c in range(C):
                        nc.scalar.activation(exp_uk[:, c], k[:, c], ACT.Exp, bias=wu[:, 1, c:c + 1])
                    a = nc.scalar.activation(y1t[:], k, ACT.Copy)
                    a.then_inc(exps_ready, 1)

            def route(b, part):
                if part == 0:
                    for c in range(C):
                        act.wait_ge(x2t_ps, C * b + (c + 1))
                        nc.scalar.activation(next_hi[:, c, :], bank[c][:, 0:TOK], ACT.Copy).then_inc(x2t_hi_ready, 1)
                if part == 1:
                    act.wait_ge(logits_t_ps, b + 1)
                    nc.scalar.activation(logits_t, bank[2][:, 0:TOK], ACT.Copy).then_inc(logits_t_ready, 1)
                if part == 3:
                    act.wait_ge(route_step, 4 * b + 2)
                    nc.scalar.activation(route_exps[:], logits[:], ACT.Exp).then_inc(route_exp, 1)
                if part == 4:
                    act.wait_ge(gate_t_ps, b + 1)
                    nc.scalar.activation(gate_t_hi[:], bank[2][0:E, 0:TOK], ACT.Copy).then_inc(gate_hi_ready, 1)

            def hidden_hi(n, g):
                act.wait_ge(gelu_done, G * n + (g + 1))
                nc.scalar.activation(h_hi[:, g, :], h_all[:, g, :], ACT.Copy).then_inc(h_hi_ready, 1)

            def hidden(n, e, g):
                act.wait_ge(up_done, G * n + (g + 1))
                for k in range(2):
                    bias = (b1_all[:, e * FC + 2 * g + k:e * FC + 2 * g + k + 1] if isinstance(e, int)
                            else b1_all[:, bass.ds(e * FC + (2 * g + k), 1)])
                    a = nc.scalar.activation(h_all[:, g, k * TOK:(k + 1) * TOK], up_ps[g % 2][:, k * TOK:(k + 1) * TOK],
                                             ACT.Gelu_apprx_tanh, bias=bias)
                a.then_inc(gelu_done, 1)
                if g > 0:
                    hidden_hi(n, g - 1)
                if g == G - 1:
                    hidden_hi(n, g)

            def move():
                nc.scalar.activation(x2t_hi[:], next_hi[:].bitcast(F32), ACT.Copy).then_inc(x2t_moved, 1)

            def split_projection(i):
                nc.scalar.activation(proj_hi[:, i], projections[:, i], ACT.Copy).then_inc(proj_hi_ready, 1)

            attend(0, X_STEP)
            for i in range(4):
                act.wait_ge(proj_loaded[i // 2], 16 * 2)
                split_projection(i)
            act.wait_ge(consts_loaded, 16 * CONSTS)
            nc.scalar.activation(bq_scaled[:], bqk[:, 0, :], ACT.Copy, scale=DH ** -0.5).then_inc(act_setup, 1)
            nc.scalar.activation(b2_hi[:], b2_raw[:], ACT.Copy).then_inc(act_setup, 1)
            act.wait_ge(dve_setup, 1)
            nc.scalar.activation(wg_hi[:, :, 0:E], wg_raw[:], ACT.Copy).then_inc(act_setup, 1)
            act.wait_ge(act_setup, 3)
            for s in FIRST_ORDER[1:]:
                attend(0, s)
                if s == V_STEP:
                    nc.scalar.activation(decay[:, 0, :], wu[:, 0, :], ACT.Exp, scale=-1.0)
                    nc.scalar.activation(decay[:, 1, :], wu[:, 0, :], ACT.Exp).then_inc(decay_ready, 1)
                if s in ROUTE_STEP:
                    route(0, ROUTE_STEP.index(s))
                if s == ROUTE_STEP[1]:
                    move()
            with act.Fori(0, NPAIR - 1) as b:
                for e in range(E):
                    for g in range(SLOTS):
                        s = e * SLOTS + g
                        if g < G:
                            hidden(b * E + e, e, g)
                        if s in GATE_STEP:
                            route(b, 4 + GATE_STEP.index(s))
                        attend(b + 1, s)
                        if s in ROUTE_STEP:
                            route(b + 1, ROUTE_STEP.index(s))
                        if s == MOVE_STEP:
                            move()
            for g in range(G):
                hidden((NPAIR - 1) * E, 0, g)
                if g in GATE_STEP:
                    route(NPAIR - 1, 4 + GATE_STEP.index(g))
            with act.Fori(1, E) as e:
                for g in range(G):
                    hidden(e + (NPAIR - 1) * E, e, g)

        @block.vector
        def _(dve):
            def low(dst, src, hi):
                return nc.vector.tensor_tensor(dst, src, hi.bitcast(F32), ALU.subtract)

            def moments_of(src, which, step, base):
                tiles = len(src)
                for j in range(tiles):
                    i = nc.vector.bn_stats(stats[:, j, :], src[j])
                i.then_inc(step, 1)
                dve.wait_ge(step, 2 * base + 1)
                nc.vector.tensor_copy(spare[:, which:which + 1], stats[:, 0, 1:2])
                for j in range(tiles):
                    i = nc.vector.bn_aggr(moments[:, which, j, :], stats[:, j, :])
                i.then_inc(step, 1)

            def norm(src, dst, which, rstd_done, base):
                dve.wait_ge(rstd_done, base + 1)
                for j in range(len(src)):
                    i = nc.vector.tensor_scalar(dst[j], src[j], moments[:, which, j, 0:1], rstd[:, which, j:j + 1],
                                                ALU.subtract, ALU.mult)
                return i

            def diagonal(p, c, part):
                if c == 0 and part == 0:
                    dve.wait_ge(k_rest_ready, p + 1)
                if c > 0 and part == 0:
                    dve.wait_ge(scores_ps, QUADS * p + 2 * PAIR * c)
                for h in (2 * part, 2 * part + 1):
                    i = nc.vector.tensor_scalar(kd[:, :, :, h, :], k_both[:, :, c, :].rearrange("p a (j t) -> p a j t", j=PAIR),
                                                head_mask[:, h:h + 1], None, ALU.mult)
                if h % HQ == HQ - 1:
                    i.then_inc(kd_ready, 1)

            def scan(i, state, inc):
                for c in range(C):
                    for j in range(PAIR):
                        o = nc.vector.tensor_tensor_scan(state[:, c, j, :], decay_row[:, i, c, :], inc[:, c, j, :],
                                                         0.0, ALU.mult, ALU.add)
                return o

            def attend(p, s):
                if s == X_STEP:
                    dve.wait_ge(xt_hi_ready, p + 1)
                    low(xt_lo[:], by_chunk(bank[0]), xt_hi[:]).then_inc(xt_ready, 1)
                if s == QK_STEP + 1:
                    dve.wait_ge(k_hi_ready, p + 1)
                    low(k_both[:, 1], k_both[:, 0], k_hi[:]).then_inc(k_rest_ready, 1)
                    dve.wait_ge(q_hi_ready, p + 1)
                    low(q_lo[:], q_all[:], q_hi[:]).then_inc(q_ready, 1)
                for c in range(C):
                    for part in range(HC // 2):
                        if s == DIAGONAL_STEP[c][part] and not (first(p) and c == 1):
                            diagonal(p, c, part)
                if s == V_STEP:
                    dve.wait_ge(v_ps, p + 1)
                    for j in range(PAIR):
                        i = nc.vector.tensor_tensor(v_all[:, j], by_tile(bank[3])[:, j], bv_all[:], ALU.add)
                    i.then_inc(v_step, 1)
                if s == VSPLIT_STEP and not first(p):
                    dve.wait_ge(v_step, 5 * p + 1)
                    nc.vector.tensor_copy(v_hi[:, :, :, 0:DH], values_by_head(v_all)).then_inc(v_step, 1)
                    dve.wait_ge(v_step, 5 * p + 2)
                    nc.vector.tensor_tensor(values_by_head(v_all), values_by_head(v_all), v_hi[:, :, :, 0:DH], ALU.subtract).then_inc(v_step, 1)
                    dve.wait_ge(v_step, 5 * p + 3)
                    nc.vector.tensor_copy(v_mid[:, :, :, 0:DH], values_by_head(v_all)).then_inc(v_step, 1)
                    dve.wait_ge(v_step, 5 * p + 4)
                    nc.vector.tensor_tensor(v_lo[:, :, :, 0:DH], values_by_head(v_all), v_mid[:, :, :, 0:DH], ALU.subtract).then_inc(v_step, 1)
                for u in range(UNITS):
                    c, j = divmod(u, PAIR)
                    if s == SCORE_STEP[u]:
                        for i in range(2):
                            g = 2 * u + i
                            dve.wait_ge(scores_ps, QUADS * p + (g + 1))
                            nc.vector.tensor_reduce(neg_max[:, g, :], by_head(score_banks(p, u)[i]), AX_X, ALU.max,
                                                    negate=True).then_inc(max_ready, 1)
                        for i in range(2):
                            g = 2 * u + i
                            dve.wait_ge(max_ready, QUADS * p + (g + 1))
                            if u >= 2:
                                dve.wait_ge(pt_ps, QUADS * p + (g - 3))
                            nc.vector.tensor_tensor(probs[:, u % 2, i], by_head(score_banks(p, u)[i]),
                                                    neg_max[:, g, :].rearrange("p (h a) -> p h a", a=1).to_broadcast([P, HQ, S]),
                                                    ALU.add).then_inc(shifted, 1)
                    if s == TURN_STEP[u]:
                        for i in range(2):
                            g = 2 * u + i
                            dve.wait_ge(pt_hi_ready, QUADS * p + (g + 1))
                            nc.vector.tensor_tensor(pt_lo[:, i], by_head(bank[2 + i]), pt_hi[:, i], ALU.subtract)\
                                .then_inc(pt_ready, 1)
                    if s == VALUE_STEP[u]:
                        dve.wait_ge(pv_ps, QUADS * p + (2 * u + 2))
                        rows = bank[u % 2][:, 0:HC * VW].rearrange("p (h e) -> p h e", h=HC)
                        nc.vector.reciprocal(inv_sum[:, u, :], rows[:, :, DH]).then_inc(inv_ready, 1)
                        dve.wait_ge(inv_ready, UNITS * p + (u + 1))
                        nc.vector.tensor_tensor(att[:, j, c * P:(c + 1) * P].rearrange("p (h e) -> p h e", h=HC), rows[:, :, 0:DH],
                                                inv_sum[:, u, :].rearrange("p (h a) -> p h a", a=1).to_broadcast([P, HC, DH]),
                                                ALU.mult).then_inc(att_ready, 1)
                if s == ATT_STEP:
                    dve.wait_ge(att_hi_ready, p + 1)
                    low(xt_lo[:], by_chunk(bank[2]), xt_hi[:]).then_inc(att_t_ready, 1)
                if s == WO_STEP:
                    dve.wait_ge(wo_ps, p + 1)
                    dve.wait_ge(x_bo_ready, p + 1)
                    nc.vector.tensor_tensor(y1[:], by_tile(bank[3]), x_bo[:], ALU.add).then_inc(y1_sum, 1)
                    dve.wait_ge(y1_sum, p + 1)
                    moments_of([y1[:, j] for j in range(PAIR)], 0, ln1_step, p)
                if s == NORM1_STEP:
                    tiles = [y1[:, j] for j in range(PAIR)]
                    norm(tiles, tiles, 0, ln1_rstd, p).then_inc(y1_ready, 1)
                if s == REC_STEP[0]:
                    dve.wait_ge(exp_minus_ready, p + 1)
                    scan(1, scan_b, inc_b).then_inc(xa_step, 1)
                    dve.wait_ge(exps_ready, p + 1)
                    dve.wait_ge(ctx_t_ready, p + 1)
                    nc.vector.tensor_tensor(inc_a[:, :, :, 2:S], exp_k[:, :, :, 1:S - 1], ctx_t[:, :, :, 1:S - 1],
                                            ALU.mult).then_inc(xa_step, 1)
                    dve.wait_ge(xa_step, 6 * p + 2)
                    scan(0, scan_a, inc_a).then_inc(xa_step, 1)
                if s == REC_STEP[1]:
                    flat = mix.rearrange("p c j t -> p (c j) t")
                    dve.wait_ge(xa_step, 6 * p + 3)
                    nc.vector.tensor_tensor(mix, ctx_t[:], scan_b[:], ALU.mult).then_inc(xa_step, 1)
                    dve.wait_ge(xa_step, 6 * p + 4)
                    nc.vector.tensor_tensor(flat, flat, ramp[:].rearrange("p (a t) -> p a t", a=1).to_broadcast([P, C * PAIR, S]),
                                            ALU.add).then_inc(xa_step, 1)
                if s == REC_STEP[2]:
                    dve.wait_ge(xa_step, 6 * p + 5)
                    nc.vector.tensor_tensor(mix, mix, exp_uk[:], ALU.mult).then_inc(xa_step, 1)
                if s == REC_STEP[3]:
                    dve.wait_ge(xa_step, 6 * p + 6)
                    dve.wait_ge(mix_a_ready, p + 1)
                    nc.vector.tensor_tensor(mix, mix, y1t[:], ALU.add).then_inc(mix_ready, 1)
                if s == BACK_STEP:
                    dve.wait_ge(x2_ps, p + 1)
                    moments_of([by_tile(bank[2])[:, j] for j in range(PAIR)], 1, ln2_step, p)
                if s == NORM2_STEP:
                    norm([by_tile(bank[2])[:, j] for j in range(PAIR)], [x2[:, j] for j in range(PAIR)], 1, ln2_rstd, p).then_inc(x2_ready, 1)

            def over_experts(v):
                return v[:].rearrange("p (t a) -> p t a", a=1).to_broadcast([P, PAIR, E])

            def route(b, part):
                if part == 0:
                    for c in range(C):
                        dve.wait_ge(x2t_hi_ready, C * b + (c + 1))
                        low(next_lo[:, c, :], bank[c][:, 0:TOK], next_hi[:, c, :]).then_inc(x2t_ready, 1)
                if part == 2:
                    dve.wait_ge(logits_ps, b + 1)
                    lg = bank[3][:, 0:PAIR * P].rearrange("p (t e) -> p t e", t=PAIR)[:, :, 0:E]
                    nc.vector.tensor_reduce(route_max[:], lg, AX_X, ALU.max, negate=True).then_inc(route_step, 1)
                    dve.wait_ge(route_step, 4 * b + 1)
                    nc.vector.tensor_tensor(logits[:], lg, over_experts(route_max), ALU.add).then_inc(route_step, 1)
                if part == 3:
                    dve.wait_ge(route_exp, b + 1)
                    nc.vector.tensor_reduce(route_sum[:], route_exps[:], AX_X, ALU.add).then_inc(route_step, 1)
                    dve.wait_ge(route_step, 4 * b + 3)
                    nc.vector.reciprocal(route_inv[:], route_sum[:]).then_inc(route_step, 1)
                    dve.wait_ge(route_step, 4 * b + 4)
                    nc.vector.tensor_tensor(next_gate[:], route_exps[:], over_experts(route_inv), ALU.mult).then_inc(gate_ready, 1)
                if part == 4:
                    dve.wait_ge(gate_hi_ready, b + 1)
                    low(gate_t_lo[:], bank[2][0:E, 0:TOK], gate_t_hi[:]).then_inc(gate_t_ready, 1)
                if part == 5:
                    dve.wait_ge(b2_ps, b + 1)
                    nc.vector.tensor_tensor(x2[:], by_tile(bank[3]), x2[:], ALU.add).then_inc(x2_biased, 1)

            def take_gates(b):
                dve.wait_ge(gate_ready, b + 1)
                nc.vector.tensor_copy(gate[:], next_gate[:]).then_inc(gates_taken, 1)

            def hidden_lo(n, g):
                dve.wait_ge(h_hi_ready, G * n + (g + 1))
                low(h_lo[:, g, :], h_all[:, g, :], h_hi[:, g, :]).then_inc(h_ready, 1)

            def add_expert(n, e, first=False):
                for t in range(PAIR):
                    dve.wait_ge(down_done, PAIR * n + (t + 1))
                    weight = gate[:, t, e:e + 1] if isinstance(e, int) else gate[:, t, bass.ds(e, 1)]
                    nc.vector.scalar_tensor_tensor(out=acc[:, t, :], in0=down_ps[t][:, 0:D], scalar=weight,
                                                   in1=x2[:, t, :] if first else acc[:, t, :],
                                                   op0=ALU.mult, op1=ALU.add).then_inc(added, 1)

            def split_w2(n, parity, half):
                dve.wait_ge(w2_loaded[parity], 16 * (half + 1))
                for g in range(G):
                    cols = slice(g * PW, (g + 1) * PW)
                    nc.vector.tensor_copy(w2_hi[:, cols], w2_raw[:, parity, cols]).then_inc(w2_hi_ready, 1)

            def split_w1(n, parity, half, groups):
                if 0 in groups:
                    dve.wait_ge(w1_loaded[parity], 16 * (half + 1))
                for g in groups:
                    nc.vector.tensor_copy(group(w1_hi[:], g), group(w1_raw[:, parity], g)).then_inc(w1_hi_ready, 1)

            def expert(n, e, g, parity, half, start=False, last=False):
                if 0 < g < G:
                    hidden_lo(n, g - 1)
                if g == G - 1:
                    hidden_lo(n, g)
                if g in W1_GROUPS and not last:
                    split_w1(n + 1, 1 - parity, half + parity, W1_GROUPS[g])
                if g == SLOTS - 1:
                    add_expert(n, e, start)
                    if not last:
                        split_w2(n + 1, 1 - parity, half + parity)

            def move():
                nc.vector.tensor_copy(x2t_lo[:], next_lo[:].bitcast(F32)).then_inc(x2t_moved, 1)

            def finish(b, part):
                tiles = [acc[:, t] for t in range(PAIR)]
                if part == 0:
                    dve.wait_ge(added, PAIR * E * (b + 1))
                    moments_of(tiles, 2, ln3_step, b)
                else:
                    norm(tiles, tiles, 2, ln3_rstd, b).then_inc(out_ready, 1)

            def split_projection(i):
                dve.wait_ge(proj_hi_ready, i + 1)
                low(proj_lo[:, i], projections[:, i], proj_hi[:, i]).then_inc(proj_ready, 1)

            nc.vector.memset(wg_hi[:].bitcast(F32), 0.0)
            nc.vector.memset(wg_lo[:].bitcast(F32), 0.0).then_inc(dve_setup, 1)
            nc.vector.memset(inc_a[:, :, :, 0:2], 0.0)
            nc.vector.memset(inc_b[:, :, :, 0:2], 0.0)
            nc.vector.memset(v_hi[:, :, :, DH:VW], 1.0)
            nc.vector.memset(v_mid[:, :, :, DH:VW], 0.0)
            nc.vector.memset(v_lo[:, :, :, DH:VW], 0.0)
            nc.vector.memset(ones[:], 1.0).then_inc(dve_setup, 1)
            dve.wait_ge(dve_setup, 2)
            nc.vector.tensor_tensor_scan(ramp[:], ones[:], ones[:], 0.0, ALU.mult, ALU.add).then_inc(dve_setup, 1)
            dve.wait_ge(dve_setup, 3)
            nc.vector.tensor_scalar(ramp[:], ramp[:], -2.0, 0.0, ALU.add, ALU.max)
            attend(0, X_STEP)
            for i in range(4):
                split_projection(i)
            dve.wait_ge(masks_made, MASKS)
            for s in FIRST_ORDER[1:]:
                attend(0, s)
                if s == Y1_STEP:
                    split_w1(0, 0, 0, range(G))
                if s == REC_STEP[-1]:
                    split_w2(0, 0, 0)
                if s == ATT_STEP:
                    dve.wait_ge(act_setup, 3)
                    low(wg_lo[:, :, 0:E], wg_raw[:], wg_hi[:, :, 0:E])
                    low(b2_lo[:], b2_raw[:], b2_hi[:]).then_inc(dve_setup, 1)
                if s == ATT_STEP:
                    dve.wait_ge(decay_ready, 1)
                    for i in range(2):
                        for c in range(C):
                            a = nc.vector.tensor_scalar(decay_row[:, i, c, :], ones[:], decay[:, i, c:c + 1], None, ALU.mult)
                    a.then_inc(dve_setup, 1)
                    dve.wait_ge(dve_setup, DVE_SETUP)
                if s in ROUTE_STEP:
                    route(0, ROUTE_STEP.index(s))
                if s == ROUTE_STEP[2]:
                    move()
            take_gates(0)
            with dve.Fori(0, NPAIR - 1) as b:
                for e in range(E):
                    for g in range(SLOTS):
                        s = e * SLOTS + g
                        if s in GATE_STEP:
                            route(b, 4 + GATE_STEP.index(s))
                        attend(b + 1, s)
                        if s == SLOTS - 1:
                            dve.wait_ge(x2_biased, b + 1)
                            dve.wait_ge(gates_taken, b + 1)
                            dve.wait_ge(acc_free, b + 1)
                        expert(b * E + e, e, g, e % 2, b * (E // 2) + e // 2, start=e == 0)
                        if s == E * SLOTS - 1:
                            finish(b, 0)
                        if s in ROUTE_STEP:
                            route(b + 1, ROUTE_STEP.index(s))
                        if s == MOVE_STEP:
                            move()
                finish(b, 1)
                take_gates(b + 1)
            first_n = (NPAIR - 1) * E
            for g in range(SLOTS):
                if g in GATE_STEP:
                    route(NPAIR - 1, 4 + GATE_STEP.index(g))
                if g == SLOTS - 1:
                    dve.wait_ge(x2_biased, NPAIR)
                    dve.wait_ge(gates_taken, NPAIR)
                    dve.wait_ge(acc_free, NPAIR)
                expert(first_n, 0, g, 0, first_n // 2, start=True)
            with dve.Fori(0, E // 2 - 1) as k:
                for j in range(1, 3):
                    for g in range(SLOTS):
                        expert(k * 2 + (first_n + j), k * 2 + j, g, j % 2, k + (first_n + j) // 2)
            for g in range(SLOTS):
                expert(NPAIR * E - 1, E - 1, g, 1, NPAIR * E // 2 - 1, last=True)
            finish(NPAIR - 1, 0)
            finish(NPAIR - 1, 1)

        @block.gpsimd
        def _(pool):
            def root(which, tiles, step, eps_done, rstd_done, base):
                pool.wait_ge(step, 2 * base + 2)
                nc.gpsimd.tensor_tensor(var_eps[:, which, 0:tiles], moments[:, which, 0:tiles, 1], eps_row[:, 0:tiles],
                                        ALU.add).then_inc(eps_done, 1)
                pool.wait_ge(eps_done, base + 1)
                nc.gpsimd.tensor_tensor(rstd[:, which, 0:tiles], var_eps[:, which, 0:tiles], power[:, 0:tiles],
                                        ALU.pow).then_inc(rstd_done, 1)

            def attend(p, s):
                if s == X_STEP:
                    pool.wait_ge(x_loaded, 16 * (p + 1))
                    if not first(p):
                        pool.wait_ge(y1_sum, p)
                    for j in range(PAIR):
                        i = nc.gpsimd.tensor_tensor(x_bo[:, j], x_in[:, j], bo_all[:], ALU.add)
                    i.then_inc(x_bo_ready, 1)
                if s == WO_STEP:
                    root(0, PAIR, ln1_step, ln1_eps, ln1_rstd, p)
                if s == VSPLIT_STEP and first(p):
                    pool.wait_ge(v_step, 1)
                    nc.gpsimd.tensor_copy(v_hi[:, :, :, 0:DH], values_by_head(v_all)).then_inc(v_step, 1)
                    pool.wait_ge(v_step, 2)
                    nc.gpsimd.tensor_tensor(values_by_head(v_all), values_by_head(v_all), v_hi[:, :, :, 0:DH], ALU.subtract).then_inc(v_step, 1)
                    pool.wait_ge(v_step, 3)
                    nc.gpsimd.tensor_copy(v_mid[:, :, :, 0:DH], values_by_head(v_all)).then_inc(v_step, 1)
                    pool.wait_ge(v_step, 4)
                    nc.gpsimd.tensor_tensor(v_lo[:, :, :, 0:DH], values_by_head(v_all), v_mid[:, :, :, 0:DH], ALU.subtract).then_inc(v_step, 1)
                if s == MIX_A_STEP:
                    pool.wait_ge(xa_step, 6 * p + 3)
                    pool.wait_ge(exps_ready, p + 1)
                    nc.gpsimd.tensor_tensor(y1t[:], y1t[:], scan_a[:], ALU.add).then_inc(mix_a_ready, 1)
                if s == BACK_STEP:
                    root(1, PAIR, ln2_step, ln2_eps, ln2_rstd, p)

            def split_w2(n, g, parity):
                pool.wait_ge(w2_hi_ready, G * n + (g + 1))
                cols = slice(g * PW, (g + 1) * PW)
                nc.gpsimd.tensor_tensor(w2_lo[:, cols], w2_raw[:, parity, cols], w2_hi[:, cols].bitcast(F32),
                                        ALU.subtract).then_inc(w2_ready, 1)

            def split_w1(n, g, parity):
                pool.wait_ge(w1_hi_ready, G * n + (g + 1))
                nc.gpsimd.tensor_tensor(group(w1_lo[:], g), group(w1_raw[:, parity], g), group(w1_hi[:], g).bitcast(F32),
                                        ALU.subtract).then_inc(w1_ready, 1)

            def expert(n, g, parity, last=False):
                if g < G - 1:
                    split_w2(n, g + 1, parity)
                elif g < SLOTS - 1 and not last:
                    split_w1(n + 1, g - (G - 1), 1 - parity)
                elif g == SLOTS - 1 and not last:
                    split_w2(n + 1, 0, 1 - parity)

            def finish(b):
                root(2, PAIR, ln3_step, ln3_eps, ln3_rstd, b)

            nc.gpsimd.memset(ident[:], 0.0).then_inc(masks_made, 1)
            nc.gpsimd.memset(head_mask[:], 1.0).then_inc(masks_made, 1)
            nc.gpsimd.memset(power[:], -0.5)
            nc.gpsimd.memset(eps_row[:], EPS).then_inc(masks_made, 1)
            pool.wait_ge(masks_made, 3)
            nc.gpsimd.affine_select(out=ident[:], in_=ident[:], compare_op=ALU.not_equal, fill=1.0,
                                    base=0, pattern=[[-1, P]], channel_multiplier=1).then_inc(masks_made, 1)
            nc.gpsimd.affine_select(out=head_mask[:], in_=head_mask[:], compare_op=ALU.is_ge, fill=0.0,
                                    base=0, pattern=[[-DH, HC]], channel_multiplier=1).then_inc(masks_made, 1)
            pool.wait_ge(masks_made, 5)
            nc.gpsimd.affine_select(out=head_mask[:], in_=head_mask[:], compare_op=ALU.is_ge, fill=0.0,
                                    base=DH - 1, pattern=[[DH, HC]], channel_multiplier=-1).then_inc(masks_made, 1)
            pool.wait_ge(consts_loaded, 16 * CONSTS)
            attend(0, X_STEP)
            for s in FIRST_ORDER[1:]:
                attend(0, s)
                if s == Y1_STEP:
                    for g in range(G):
                        split_w1(0, g, 0)
            split_w2(0, 0, 0)
            with pool.Fori(0, NPAIR - 1) as b:
                for e in range(E):
                    for g in range(SLOTS):
                        attend(b + 1, e * SLOTS + g)
                        expert(b * E + e, g, e % 2)
                finish(b)
            first_n = (NPAIR - 1) * E
            for g in range(SLOTS):
                expert(first_n, g, 0)
            with pool.Fori(0, E // 2 - 1) as k:
                for j in range(1, 3):
                    for g in range(SLOTS):
                        expert(k * 2 + (first_n + j), g, j % 2)
            for g in range(SLOTS):
                expert(NPAIR * E - 1, g, 1, last=True)
            finish(NPAIR - 1)


X_STEP, QK_STEP, V_STEP, VSPLIT_STEP = 1, 3, 5, 13
SCORE_STEP = [8, 10, 24, 26]
EXP_STEP = [12, 13, 28, 29]
TURN_STEP = [14, 17, 30, 32]
VALUE_STEP = [16, 19, 31, 34]
ATT_STEP, CTX_STEP, WO_STEP, NORM1_STEP, Y1_STEP = 36, 37, 38, 40, 42
XEXP_STEP, MIX_A_STEP, BACK_STEP, NORM2_STEP = 44, 51, 54, 56
DIAGONAL_STEP = [[4, 4, 5, 5], [19, 20, 21, 22]]
REC_STEP = [48, 50, 51, 52]
ROUTE_STEP = [58, 60, 61, 62]
MOVE_STEP = 61
GATE_STEP = [0, 3]
W1_GROUPS = {3: [0], 4: [1, 2, 3]}
FIRST_ORDER = ([X_STEP, QK_STEP, QK_STEP + 1, V_STEP, SCORE_STEP[0], SCORE_STEP[1], SCORE_STEP[2],
                EXP_STEP[0], EXP_STEP[1], TURN_STEP[0], EXP_STEP[2], SCORE_STEP[3], VALUE_STEP[0],
                TURN_STEP[1], VALUE_STEP[1], EXP_STEP[3], TURN_STEP[2], VALUE_STEP[2], TURN_STEP[3], VALUE_STEP[3]]
               + list(range(ATT_STEP, ROUTE_STEP[-1] + 1)))
MASKS = 6
DVE_SETUP = 5


def kernel(**inputs):
    import numpy as _np
    import concourse.bacc as _bacc
    from concourse.bass_utils import run_bass_kernel_spmd as _run

    a = {k.replace("L0_", ""): _np.asarray(v) for k, v in inputs.items()}
    D = a["x"].shape[2]
    E, F = a["ffn_b1"].shape
    by_in = lambda w: w.transpose(1, 0, 2).reshape(D, D)
    laid = {
        "x": a["x"], "ctx": a["ctx_1024"],
        "wq": by_in(a["attn_wq"]), "wk": by_in(a["attn_wk"]), "wv": by_in(a["attn_wv"]), "wo": a["attn_wo"].T,
        "cols": _np.stack([a[k].reshape(D // 128, 128).T for k in ("attn_bq", "attn_bk", "xattn_w", "xattn_u")], axis=1),
        "bv": a["attn_bv"].reshape(D), "bo": a["attn_bo"],
        "wg": a["ffn_Wg"].T.reshape(D // 128, 128, E),
        "w1": a["ffn_W1"],
        "b1": a["ffn_b1"].reshape(E, F // 128, 128).transpose(2, 0, 1).reshape(128, E * F // 128),
        "w2": a["ffn_W2"], "b2": a["ffn_b2"],
    }
    nc = _bacc.Bacc("TRN2", target_bir_lowering=False, num_devices=1)
    arrays, args = {}, []
    for name, v in laid.items():
        arrays[f"in_{name}_dram"] = _np.ascontiguousarray(v)
        args.append(nc.dram_tensor(f"in_{name}_dram", v.shape, mybir.dt.from_np(v.dtype), kind="ExternalInput").ap())
    out = nc.dram_tensor("out_dram", a["x"].shape, F32, kind="ExternalOutput").ap()
    decoder_layer(nc, *args, out)
    return _run(nc, [arrays], core_ids=[0]).results[0]["out_dram"]
```
